# Optimizing a Trainium2 kernel written in Bass

```python
import numpy as np
import jax
import jax.numpy as jnp

def _softmax(x, axis=-1):
    return jax.nn.softmax(x, axis=axis)

def _gelu(x):
    return jax.nn.gelu(x, approximate=True)

def _silu(x):
    return jax.nn.silu(x)

def _sigmoid(x):
    return jax.nn.sigmoid(x)

def _layernorm(x, axis=-1, eps=1e-05):
    m = jnp.mean(x, axis=axis, keepdims=True)
    v = jnp.var(x, axis=axis, keepdims=True)
    return (x - m) / jnp.sqrt(v + eps)

def _scatter_add(tgt, idx, src, axis=0):
    return tgt.at[idx].add(src)

def _segment_sum(src, seg, n):
    return jax.ops.segment_sum(src, seg, n)
kernel_name = 'mk_gps_d1_gnn_r8_2e20fa'

def setup_inputs(seed: int=0):
    np.random.seed(seed)
    _w = jnp.asarray

    def _rec_inputs():
        import jax
        import jax.numpy as jnp
        _gk = jax.random.key(seed)
        x = -0.0002117 + 1 * jax.random.normal(jax.random.fold_in(_gk, 1), (12500, 256), jnp.float32)
        _s = jax.random.randint(jax.random.fold_in(_gk, 2), (100000,), 0, 12500, jnp.int32)
        _d = jax.random.randint(jax.random.fold_in(_gk, 3), (100000,), 0, 12500, jnp.int32)
        _loop = jnp.arange(12500, dtype=jnp.int32)
        src = jnp.concatenate([_s, _d, _loop])
        dst = jnp.concatenate([_d, _s, _loop])
        _o = jnp.argsort(dst, stable=True)
        src = src[_o]
        dst = dst[_o]
        edge_weight = jax.random.uniform(jax.random.fold_in(_gk, 12), (212500,), jnp.float32, 0.0, 1)
        return (x, src, dst, edge_weight)
    x, src, dst, edge_weight = _rec_inputs()

    def _L0_gnn_setup():
        import jax, jax.numpy as jnp
        import numpy as np
        N = 12500
        E = 200000
        D_IN = 256
        D_OUT = 256
        key = jax.random.key(seed)
        ks = jax.random.split(key, 8)
        stdv1 = 1.0 / np.sqrt(D_IN)
        stdv2 = 1.0 / np.sqrt(D_OUT)
        return {'x': jax.random.normal(ks[0], (N, D_IN), dtype=jnp.float32), 'edge_val': jax.random.uniform(ks[1], (E,), dtype=jnp.float32), 'W1': jax.random.uniform(ks[2], (D_OUT, D_IN), minval=-stdv1, maxval=stdv1, dtype=jnp.float32), 'b1': jax.random.uniform(ks[3], (D_OUT,), minval=-stdv1, maxval=stdv1, dtype=jnp.float32), 'W2': jax.random.uniform(ks[4], (D_OUT, D_OUT), minval=-stdv2, maxval=stdv2, dtype=jnp.float32), 'b2': jax.random.uniform(ks[5], (D_OUT,), minval=-stdv2, maxval=stdv2, dtype=jnp.float32), 'eps': jnp.zeros((1,), dtype=jnp.float32), 'edge_src': jax.random.randint(ks[6], (E,), 0, N, dtype=jnp.int32), 'edge_dst': jax.random.randint(ks[7], (E,), 0, N, dtype=jnp.int32)}
    _L0_gnn_all = _L0_gnn_setup()
    _L0_gnn_in = {k: v for k, v in _L0_gnn_all.items() if k in ('W1', 'b1', 'W2', 'b2', 'eps')}
    del _L0_gnn_all

    def _L0_mix_setup():
        import jax, jax.numpy as jnp
        import numpy as np
        C_CURV = 1.0
        MIN_NORM = 1e-15
        BALL_EPS = 1e-05
        ATT_EPS = 1e-15
        DIM = 32

        def _norm(x):
            return jnp.clip(jnp.linalg.norm(x, axis=-1, keepdims=True), MIN_NORM)

        def proj(x, c):
            maxnorm = (1.0 - BALL_EPS) / jnp.sqrt(c)
            n = _norm(x)
            return jnp.where(n > maxnorm, x / n * maxnorm, x)

        def expmap0(u, c):
            sc = jnp.sqrt(c)
            n = _norm(u)
            return jnp.tanh(sc * n) * u / (sc * n)

        def logmap0(p, c):
            sc = jnp.sqrt(c)
            n = _norm(p)
            return jnp.arctanh(jnp.clip(sc * n, -1.0 + 1e-07, 1.0 - 1e-07)) * p / (sc * n)

        def mobius_add(x, y, c):
            x2 = jnp.sum(x * x, -1, keepdims=True)
            y2 = jnp.sum(y * y, -1, keepdims=True)
            xy = jnp.sum(x * y, -1, keepdims=True)
            num = (1 + 2 * c * xy + c * y2) * x + (1 - c * x2) * y
            den = 1 + 2 * c * xy + c * c * x2 * y2
            return num / jnp.clip(den, MIN_NORM)

        def conv1d(x, w, pad, groups=1):
            return jax.lax.conv_general_dilated(x, w, (1,), [(pad, pad)], dimension_numbers=('NCH', 'OIH', 'NCH'), feature_group_count=groups)

        def batchnorm(x, gamma, beta):
            mean = jnp.mean(x, axis=(0, 2), keepdims=True)
            var = jnp.var(x, axis=(0, 2), keepdims=True)
            xn = (x - mean) * jax.lax.rsqrt(var + 1e-05)
            return gamma[None, :, None] * xn + beta[None, :, None]

        def _reference_tuple_inner(x, w_qkv, bn_gamma, bn_beta, w_dw, w_pw, w_res, b_res):
            c = C_CURV
            h = logmap0(proj(x, c), c)
            h = jnp.transpose(h, (1, 2, 0))
            h = conv1d(h, w_qkv, pad=2)
            h = batchnorm(h, bn_gamma, bn_beta)
            h = jax.nn.relu(jnp.transpose(h, (2, 0, 1)))
            qkv = proj(expmap0(h, c), c)
            t = jnp.transpose(logmap0(proj(qkv, c), c), (1, 2, 0))
            s = conv1d(t, w_dw, pad=2, groups=t.shape[1])
            s = conv1d(s, w_pw, pad=0, groups=t.shape[1] // DIM)
            cat = jnp.concatenate([t, s], axis=1)
            ai = proj(expmap0(jnp.transpose(cat, (2, 0, 1)), c), c)
            t2 = logmap0(proj(ai, c), c)
            L, N, C2 = t2.shape
            g = C2 // (3 * DIM)
            qkv3 = jnp.transpose(t2, (1, 2, 0)).reshape(N, g, 3 * DIM, L)
            q, k, v = jnp.split(qkv3, 3, axis=2)
            q = jax.nn.relu(q)
            k = jax.nn.relu(k)
            vk = jnp.einsum('ngdl,ngel->ngde', v, k)
            out = jnp.einsum('ngde,ngdl->ngdl', vk, q)
            out = out / (jnp.sum(v, -1, keepdims=True) + ATT_EPS)
            out = jnp.transpose(out.reshape(N, g * DIM, L), (2, 0, 1))
            fx_h = proj(expmap0(out, c), c)
            ft = jnp.transpose(logmap0(proj(fx_h, c), c), (1, 2, 0))
            ft = conv1d(ft, w_res, pad=0) + b_res[None, :, None]
            fx = proj(expmap0(jnp.transpose(ft, (2, 0, 1)), c), c)
            residual = mobius_add(fx, x, c)
            return (fx, residual)
        key = jax.random.key(seed)
        ks = jax.random.split(key, 6)
        L, N, C, TD = (256, 16, 256, 256)
        x = jax.random.normal(ks[0], (L, N, C), jnp.float32) * 0.05
        w_qkv = jax.random.normal(ks[1], (3 * TD, C, 5), jnp.float32) / np.sqrt(C * 5)
        bn_gamma = jnp.ones((3 * TD,), jnp.float32)
        bn_beta = jnp.zeros((3 * TD,), jnp.float32)
        w_dw = jax.random.normal(ks[2], (3 * TD, 1, 5), jnp.float32) / np.sqrt(5.0)
        w_pw = jax.random.normal(ks[3], (3 * TD, DIM, 1), jnp.float32) / np.sqrt(DIM)
        w_res = jax.random.normal(ks[4], (C, 2 * TD, 1), jnp.float32) / np.sqrt(2 * TD)
        b_res = jnp.zeros((C,), jnp.float32)
        return {'x': x, 'w_qkv': w_qkv, 'bn_gamma': bn_gamma, 'bn_beta': bn_beta, 'w_dw': w_dw, 'w_pw': w_pw, 'w_res': w_res, 'b_res': b_res}
    _L0_mix_all = _L0_mix_setup()
    _L0_mix_in = {k: v for k, v in _L0_mix_all.items() if k in ('w_qkv', 'bn_gamma', 'bn_beta', 'w_dw', 'w_pw', 'w_res', 'b_res')}
    del _L0_mix_all

    def _L0_ffn_setup():
        import jax, jax.numpy as jnp
        import numpy as np
        B, S, D = (8, 512, 256)
        H = 4 * D
        CAPACITY = 0.5
        key = jax.random.key(seed)
        ks = jax.random.split(key, 6)
        x = jax.random.normal(ks[0], (B, S, D), dtype=jnp.float32)
        attention_mask = jnp.zeros((B, 1, 1, S), dtype=jnp.float32)
        wr = jax.random.normal(ks[1], (D, 1), dtype=jnp.float32) * 0.02
        br = jnp.zeros((1,), dtype=jnp.float32)
        w1 = jax.random.normal(ks[2], (D, H), dtype=jnp.float32) * 0.02
        b1 = jnp.zeros((H,), dtype=jnp.float32)
        w2 = jax.random.normal(ks[3], (H, D), dtype=jnp.float32) * 0.02
        b2 = jnp.zeros((D,), dtype=jnp.float32)
        return {'x': x, 'attention_mask': attention_mask, 'wr': wr, 'br': br, 'w1': w1, 'b1': b1, 'w2': w2, 'b2': b2}
    _L0_ffn_all = _L0_ffn_setup()
    _L0_ffn_in = {k: v for k, v in _L0_ffn_all.items() if k in ('attention_mask', 'wr', 'br', 'w1', 'b1', 'w2', 'b2')}
    del _L0_ffn_all
    return {'x': x, 'src': src, 'dst': dst, 'edge_weight': edge_weight, 'L0_gnn_W1': _L0_gnn_in['W1'], 'L0_gnn_b1': _L0_gnn_in['b1'], 'L0_gnn_W2': _L0_gnn_in['W2'], 'L0_gnn_b2': _L0_gnn_in['b2'], 'L0_gnn_eps': _L0_gnn_in['eps'], 'L0_mix_w_qkv': _L0_mix_in['w_qkv'], 'L0_mix_bn_gamma': _L0_mix_in['bn_gamma'], 'L0_mix_bn_beta': _L0_mix_in['bn_beta'], 'L0_mix_w_dw': _L0_mix_in['w_dw'], 'L0_mix_w_pw': _L0_mix_in['w_pw'], 'L0_mix_w_res': _L0_mix_in['w_res'], 'L0_mix_b_res': _L0_mix_in['b_res'], 'L0_ffn_attention_mask': _L0_ffn_in['attention_mask'], 'L0_ffn_wr': _L0_ffn_in['wr'], 'L0_ffn_br': _L0_ffn_in['br'], 'L0_ffn_w1': _L0_ffn_in['w1'], 'L0_ffn_b1': _L0_ffn_in['b1'], 'L0_ffn_w2': _L0_ffn_in['w2'], 'L0_ffn_b2': _L0_ffn_in['b2']}

def reference(x, src, dst, edge_weight, L0_gnn_W1, L0_gnn_b1, L0_gnn_W2, L0_gnn_b2, L0_gnn_eps, L0_mix_w_qkv, L0_mix_bn_gamma, L0_mix_bn_beta, L0_mix_w_dw, L0_mix_w_pw, L0_mix_w_res, L0_mix_b_res, L0_ffn_attention_mask, L0_ffn_wr, L0_ffn_br, L0_ffn_w1, L0_ffn_b1, L0_ffn_w2, L0_ffn_b2):
    import jax
    import jax.numpy as jnp

    def _L0_gnn_ref(x, edge_val, W1, b1, W2, b2, eps, edge_src, edge_dst):
        import jax, jax.numpy as jnp
        import numpy as np
        N = 12500
        E = 200000
        D_IN = 256
        D_OUT = 256
        msgs = edge_val[:, None] * x[edge_src]
        agg = jax.ops.segment_sum(msgs, edge_dst, num_segments=N)
        support = (1.0 + eps) * x + agg
        h = jax.nn.relu(support @ W1.T + b1)
        return h @ W2.T + b2

    def _L0_mix_ref(x, w_qkv, bn_gamma, bn_beta, w_dw, w_pw, w_res, b_res):
        import jax, jax.numpy as jnp
        import numpy as np
        C_CURV = 1.0
        MIN_NORM = 1e-15
        BALL_EPS = 1e-05
        ATT_EPS = 1e-15
        DIM = 32

        def _norm(x):
            return jnp.clip(jnp.linalg.norm(x, axis=-1, keepdims=True), MIN_NORM)

        def proj(x, c):
            maxnorm = (1.0 - BALL_EPS) / jnp.sqrt(c)
            n = _norm(x)
            return jnp.where(n > maxnorm, x / n * maxnorm, x)

        def expmap0(u, c):
            sc = jnp.sqrt(c)
            n = _norm(u)
            return jnp.tanh(sc * n) * u / (sc * n)

        def logmap0(p, c):
            sc = jnp.sqrt(c)
            n = _norm(p)
            return jnp.arctanh(jnp.clip(sc * n, -1.0 + 1e-07, 1.0 - 1e-07)) * p / (sc * n)

        def mobius_add(x, y, c):
            x2 = jnp.sum(x * x, -1, keepdims=True)
            y2 = jnp.sum(y * y, -1, keepdims=True)
            xy = jnp.sum(x * y, -1, keepdims=True)
            num = (1 + 2 * c * xy + c * y2) * x + (1 - c * x2) * y
            den = 1 + 2 * c * xy + c * c * x2 * y2
            return num / jnp.clip(den, MIN_NORM)

        def conv1d(x, w, pad, groups=1):
            return jax.lax.conv_general_dilated(x, w, (1,), [(pad, pad)], dimension_numbers=('NCH', 'OIH', 'NCH'), feature_group_count=groups)

        def batchnorm(x, gamma, beta):
            mean = jnp.mean(x, axis=(0, 2), keepdims=True)
            var = jnp.var(x, axis=(0, 2), keepdims=True)
            xn = (x - mean) * jax.lax.rsqrt(var + 1e-05)
            return gamma[None, :, None] * xn + beta[None, :, None]

        def _reference_tuple_inner(x, w_qkv, bn_gamma, bn_beta, w_dw, w_pw, w_res, b_res):
            c = C_CURV
            h = logmap0(proj(x, c), c)
            h = jnp.transpose(h, (1, 2, 0))
            h = conv1d(h, w_qkv, pad=2)
            h = batchnorm(h, bn_gamma, bn_beta)
            h = jax.nn.relu(jnp.transpose(h, (2, 0, 1)))
            qkv = proj(expmap0(h, c), c)
            t = jnp.transpose(logmap0(proj(qkv, c), c), (1, 2, 0))
            s = conv1d(t, w_dw, pad=2, groups=t.shape[1])
            s = conv1d(s, w_pw, pad=0, groups=t.shape[1] // DIM)
            cat = jnp.concatenate([t, s], axis=1)
            ai = proj(expmap0(jnp.transpose(cat, (2, 0, 1)), c), c)
            t2 = logmap0(proj(ai, c), c)
            L, N, C2 = t2.shape
            g = C2 // (3 * DIM)
            qkv3 = jnp.transpose(t2, (1, 2, 0)).reshape(N, g, 3 * DIM, L)
            q, k, v = jnp.split(qkv3, 3, axis=2)
            q = jax.nn.relu(q)
            k = jax.nn.relu(k)
            vk = jnp.einsum('ngdl,ngel->ngde', v, k)
            out = jnp.einsum('ngde,ngdl->ngdl', vk, q)
            out = out / (jnp.sum(v, -1, keepdims=True) + ATT_EPS)
            out = jnp.transpose(out.reshape(N, g * DIM, L), (2, 0, 1))
            fx_h = proj(expmap0(out, c), c)
            ft = jnp.transpose(logmap0(proj(fx_h, c), c), (1, 2, 0))
            ft = conv1d(ft, w_res, pad=0) + b_res[None, :, None]
            fx = proj(expmap0(jnp.transpose(ft, (2, 0, 1)), c), c)
            residual = mobius_add(fx, x, c)
            return (fx, residual)
        return _reference_tuple_inner(x, w_qkv, bn_gamma, bn_beta, w_dw, w_pw, w_res, b_res)[0]

    def _L0_ffn_ref(x, attention_mask, wr, br, w1, b1, w2, b2):
        import jax, jax.numpy as jnp
        import numpy as np
        B, S, D = (8, 512, 256)
        H = 4 * D
        CAPACITY = 0.5
        b, s, d = x.shape
        weights = (jnp.einsum('bsd,do->bso', x, wr) + br)[..., 0]
        k = max(1, int(CAPACITY * s))
        kk = k - 1 if k > 1 else 1
        _, idx = jax.lax.top_k(weights, k)
        sel_idx = idx[:, :kk]
        sel = jnp.take_along_axis(x, sel_idx[:, :, None], axis=1)
        h = jax.nn.gelu(jnp.einsum('bkd,dh->bkh', sel, w1) + b1)
        y = jnp.einsum('bkh,hd->bkd', h, w2) + b2
        w_sel = jnp.take_along_axis(weights, sel_idx, axis=1)
        y = y * w_sel[..., None]
        batch_idx = jnp.arange(b)[:, None]
        processed = jnp.zeros_like(x).at[batch_idx, sel_idx].set(y)
        return processed + x
    xn = _layernorm(x, axis=-1)
    x = x + _L0_gnn_ref(xn, edge_weight, L0_gnn_W1, L0_gnn_b1, L0_gnn_W2, L0_gnn_b2, L0_gnn_eps, src, dst) + _L0_mix_ref(xn[None], L0_mix_w_qkv, L0_mix_bn_gamma, L0_mix_bn_beta, L0_mix_w_dw, L0_mix_w_pw, L0_mix_w_res, L0_mix_b_res)[0]
    x = x + _L0_ffn_ref(_layernorm(x, axis=-1)[None], L0_ffn_attention_mask, L0_ffn_wr, L0_ffn_br, L0_ffn_w1, L0_ffn_b1, L0_ffn_w2, L0_ffn_b2)[0]
    return x

_drawn_inputs = setup_inputs


def setup_inputs(seed=0):
    import zlib

    import numpy as np

    out = dict(_drawn_inputs(seed))
    spreads = {'L0_mix_bn_gamma': (1.0, 0.6),
     'L0_mix_bn_beta': (0.0, 0.574),
     'L0_mix_b_res': (0.0, 0.441),
     'L0_ffn_b1': (0.0, 0.8),
     'L0_ffn_b2': (0.0, 0.8)}
    factors = {'L0_gnn_b1': 4.91,
     'L0_mix_w_dw': 8.0,
     'L0_mix_w_pw': 8.0,
     'L0_ffn_wr': 4.852,
     'L0_ffn_w1': 6.794,
     'L0_ffn_w2': 6.434}
    for name, (base, spread) in spreads.items():
        noise = np.random.default_rng([zlib.crc32(name.encode()), seed]).standard_normal(out[name].shape)
        drawn = base * np.exp(spread * noise) if base else spread * noise
        out[name] = jnp.asarray(drawn.astype(out[name].dtype))
    for name, factor in factors.items():
        out[name] = (out[name] * factor).astype(out[name].dtype)
    return out
```

```python
from contextlib import ExitStack

import numpy as np
import concourse.bass as bass
from concourse import mybir

ALU = mybir.AluOpType
ACT = mybir.ActivationFunctionType
F32 = mybir.dt.float32
I32 = mybir.dt.int32
AX_X = mybir.AxisListType.X

P = 128
D = 256
C = 2
QC = 6
HID = 1024
HC = HID // P
RING = 12
LEAD = 10
G = 7
LN_EPS = 1e-5
TINY = 1e-18
BALL = float(np.float32(1.0 - 1e-5))
AMAX = float(np.arctanh(np.float64(np.float32(1.0 - 1e-5))))
ATT_EPS = 1e-15
BIG = 1.0e6
LOWEST = -3.0e38


class Link:

    def __init__(self, eng, sem, per, i):
        self.eng, self.sem, self.per, self.n, self.i = eng, sem, per, 0, i

    def __call__(self, ins):
        self.n += 1
        ins.then_inc(self.sem, 1)
        self.eng.wait_ge(self.sem, self.i * self.per + self.n)

    def close(self):
        assert self.n == self.per, (self.n, self.per)


def build(nc, a, out):
    x, src, dst, ew = a["x"], a["src"], a["dst"], a["edge_weight"]
    N, E = x.shape[0], src.shape[0]
    NT = -(-N // P)
    NS = NT // 2
    LAST = N - (NT - 1) * P
    ET = -(-E // P)
    EC = -(-ET // P)
    FULL, TAIL = E // P, E % P
    SLOTS = -(-E // (NT * P)) + 1
    STEP_SLOTS = 2 * SLOTS
    TURNS = STEP_SLOTS // RING
    TW = EC * P + SLOTS + 1
    TOP = N // 2 - 1
    QT = -(-TOP // P)
    QW = QT + (QT % 2)
    assert NT % (2 * G) == 0 and STEP_SLOTS % RING == 0 and TAIL

    with ExitStack() as ctx:
        def sb(name, shape, dt=F32):
            return ctx.enter_context(nc.sbuf_tensor(name, shape, dt))

        def psum(name, shape, dt=F32):
            return ctx.enter_context(nc.psum_tensor(name, shape, dt))

        def sem(name):
            return ctx.enter_context(nc.semaphore(name))

        def dram(name, shape, dt=F32):
            return nc.dram_tensor(name, shape, dt, kind="Internal").ap()

        xn_dram = dram("xn_dram", (NT * P, D))
        pair_dram = dram("pair_dram", (NT * P, 2 * D))
        tile_ends_dram = dram("tile_ends_dram", (2, EC, P))
        bounds_dram = dram("bounds_dram", (NT, 4), I32)

        resident = sb("resident", [P, C * NT * P])
        h0T = resident[:, :].rearrange("p (c n) -> p c n", c=C)
        srcT = sb("srcT", [P, TW])
        dstT = sb("dstT", [P, TW])
        ewT = sb("ewT", [P, TW])
        msg = [sb(f"msg{s}", [P, D]) for s in range(RING)]
        sel = [sb(f"sel{s}", [P, P]) for s in range(RING)]
        src_stage = [sb(f"src_stage{h}", [P, SLOTS + 1], I32) for h in range(2)]
        rem_msg = sb("rem_msg", [P, D])
        rem_sel = sb("rem_sel", [P, P])
        rem_src = sb("rem_src", [P, 1], I32)
        bounds = sb("bounds", [1, 4 * NT], I32)
        ident = sb("ident", [P, P])
        zeros = sb("zeros", [P, P])
        ones = sb("ones", [P, P])
        below = sb("below", [P, P])
        iota = sb("iota", [P, P])
        tile_col = sb("tile_col", [P, NT])
        iota_t = [sb(f"iota_t{h}", [P, P]) for h in range(2)]
        wqkvT = sb("wqkvT", [P, C, QC * P])
        mixW = sb("mixW", [P, QC, P])
        wresT = sb("wresT", [P, 4, D])
        w1T = sb("w1T", [P, C, D])
        w2T = sb("w2T", [P, C, D])
        b2_row = sb("b2_row", [P, D])
        bres_row = sb("bres_row", [P, D])
        wr_row = sb("wr_row", [P, D])
        cols = sb("cols", [P, 64])
        b1_col, br_col, eps_col, eps1_col = cols[:, 0:2], cols[:, 2:3], cols[:, 3:4], cols[:, 4:5]
        gam, bet, wdw = cols[:, 8:14], cols[:, 14:20], cols[:, 20:26]
        bn_a, bn_b = cols[:, 26:32], cols[:, 32:38]
        att_eps_col, tiny_col = cols[:, 38:39], cols[:, 39:40]
        h0_sums = sb("h0_sums", [P, C, NT])
        route_w = sb("route_w", [P, NT])
        work = sb("work", [P, 10688])

        def view(base, at, *shape):
            n = 1
            for s in shape:
                n *= s
            v = base[:, at:at + n]
            if len(shape) == 2:
                v = v.rearrange("p (a b) -> p a b", b=shape[1])
            if len(shape) == 3:
                v = v.rearrange("p (a b c) -> p a b c", b=shape[1], c=shape[2])
            return v

        banks = [psum(f"bank{b}", [P, 512]) for b in range(5)]
        qkv = psum("qkv", [P, 3, 2, 2, P])
        agg = banks[3:5]

        params_landed = sem("params_landed")
        consts_ready = sem("consts_ready")
        block = ctx.enter_context(nc.Block())

        rows = view(resident, 0, 3, EC, P)
        ends_bc = view(resident, 5000, 2, EC * P)
        iota_m = view(resident, 5000 + 2 * EC * P, EC * P)
        tmp_m = view(resident, 5000 + 3 * EC * P, EC * P)
        ends = view(resident, 12000, 2, EC)
        endsT = view(resident, 12100, 2, P)
        lohi = view(resident, 12400, 4)
        lohi_i = view(resident, 12410, 4).bitcast(I32)
        thr = view(resident, 12420, 1)
        rows_clear, rows_landed, rows_float = sem("rows_clear"), sem("rows_landed"), sem("rows_float")
        row_turned, table_col = sem("row_turned"), sem("table_col")
        ends_ready, ends_turned, ends_out, ends_stored, ends_landed = (
            sem("ends_ready"), sem("ends_turned"), sem("ends_out"), sem("ends_stored"), sem("ends_landed"))
        bounds_ready, bounds_stored, bounds_landed = sem("bounds_ready"), sem("bounds_stored"), sem("bounds_landed")
        table_link = sem("table_link")
        n_row_loads = 3 * (EC + 1)

        def tables_sync(sp):
            sp.wait_ge(rows_clear, 1)
            for k, arr in enumerate((src, dst, ew)):
                t = rows[:, k] if k == 2 else rows[:, k].bitcast(I32)
                for c in range(EC):
                    n = min(P, FULL - c * P)
                    sp.dma_start(t[:n, c, :], arr[c * P * P:(c * P + n) * P].rearrange("(p j) -> p j", j=P)
                                 ).then_inc(rows_landed, 16)
                    if n < P:
                        sp.dma_start(t[n:n + 1, c, :TAIL], arr[FULL * P:E].rearrange("(p j) -> p j", p=1)
                                     ).then_inc(rows_landed, 16)
            sp.wait_ge(ends_out, 2)
            for k in range(2):
                sp.dma_start(tile_ends_dram[k], endsT[:EC, k, :]).then_inc(ends_stored, 16)
            sp.wait_ge(ends_stored, 32)
            sp.dma_start(ends_bc[:NT], tile_ends_dram.rearrange("k c j -> k (c j)").partition_broadcast(NT)
                         ).then_inc(ends_landed, 16)
            sp.wait_ge(bounds_ready, 1)
            sp.dma_start(bounds_dram, lohi_i[:NT]).then_inc(bounds_stored, 16)
            sp.wait_ge(bounds_stored, 16)
            sp.dma_start(bounds[:, :], bounds_dram.rearrange("t k -> (t k)").rearrange("(a n) -> a n", a=1)
                         ).then_inc(bounds_landed, 16)

        def params_act(act):
            def load(dst_ap, src_ap):
                act.dma_start(dst_ap, src_ap).then_inc(params_landed, 16)

            load(wqkvT[:, :, :], a["wqkvT"][2].rearrange("(c p) o -> p c o", p=P))
            act.wait_ge(consts_ready, 9)
            for g in range(4):
                load(mixW[32 * g:32 * g + 32, :, 32 * g:32 * g + 32], a["w_pw"][g])
            load(wresT[:, :, :], a["wresT"].rearrange("(c p) o -> p c o", p=P))
            load(w1T[:, :, :], a["W1T"].rearrange("(c p) o -> p c o", p=P))
            load(w2T[:, :, :], a["W2T"].rearrange("(c p) o -> p c o", p=P))
            load(b2_row[:, :], a["b2"].partition_broadcast(P))
            load(bres_row[:, :], a["b_res"].partition_broadcast(P))
            load(wr_row[:, :], a["wr"].partition_broadcast(P))
            load(b1_col, a["b1"])
            load(br_col, a["br"].partition_broadcast(P))
            load(eps_col, a["eps"].partition_broadcast(P))
            load(gam, a["gamma"])
            load(bet, a["beta"])
            load(wdw, a["w_dw"][2])

        n_params = 1 + 4 + 3 + 3 + 3 + 3

        def tables_pool(pool):
            g = nc.gpsimd
            g.iota(iota[:, :], [[1, P]], base=0, channel_multiplier=0,
                   allow_small_or_imprecise_dtypes=True).then_inc(consts_ready, 1)
            g.iota(tile_col[:, :], [[P, NT]], base=0, channel_multiplier=0,
                   allow_small_or_imprecise_dtypes=True).then_inc(consts_ready, 1)
            g.iota(iota_m, [[1, EC * P]], base=0, channel_multiplier=0,
                   allow_small_or_imprecise_dtypes=True).then_inc(consts_ready, 1)
            g.iota(thr, [[0, 1]], base=0, channel_multiplier=P,
                   allow_small_or_imprecise_dtypes=True).then_inc(consts_ready, 1)
            g.memset(zeros[:, :], 0.0).then_inc(consts_ready, 1)
            g.memset(ones[:, :], 1.0).then_inc(consts_ready, 1)
            pool.wait_ge(consts_ready, 6)
            g.affine_select(out=ident[:, :], in_=zeros[:, :], compare_op=ALU.not_equal, fill=1.0, base=0,
                            pattern=[[-1, P]], channel_multiplier=1).then_inc(consts_ready, 1)
            g.affine_select(out=below[:, :], in_=ones[:, :], compare_op=ALU.is_gt, fill=0.0, base=0,
                            pattern=[[1, P]], channel_multiplier=-1).then_inc(consts_ready, 1)
            g.memset(mixW[:, :, :], 0.0).then_inc(consts_ready, 1)

        N_CONST = 9

        def counted(eng, s, reg, by=1):
            eng.wait_ge(s, eng.snap(reg, min_val=1, max_val=1 << 20))
            eng.reg_add(reg, reg, by)

        def tables_vector(dve):
            v = nc.vector
            link = Link(dve, table_link, 7, 0)
            v.memset(rows[:, 0].bitcast(I32), 0)
            v.memset(rows[:, 1].bitcast(I32), int(BIG))
            v.memset(rows[:, 2], 0.0).then_inc(rows_clear, 1)
            v.memset(srcT[:, :], 0.0)
            v.memset(dstT[:, :], -1.0)
            v.memset(att_eps_col, ATT_EPS)
            v.memset(tiny_col, TINY)
            link(v.memset(ewT[:, :], 0.0))
            dve.wait_ge(rows_landed, 16 * n_row_loads)
            v.tensor_copy(rows[:, 0:2], rows[:, 0:2].bitcast(I32)).then_inc(rows_float, 1)
            dve.wait_ge(rows_float, 1)
            v.tensor_reduce(ends[:, 0, :], rows[:, 1], AX_X, ALU.max)
            v.tensor_reduce(ends[:, 1, :], rows[:, 1], AX_X, ALU.min).then_inc(ends_ready, 1)
            for k in range(2):
                dve.wait_ge(ends_turned, k + 1)
                v.tensor_copy(endsT[:EC, k, :], banks[k][0:EC, 0:P]).then_inc(ends_out, 1)
            for k in range(3 * EC):
                dve.wait_ge(row_turned, k + 1)
                v.tensor_copy((srcT, dstT, ewT)[k // EC][:, (k % EC) * P:(k % EC + 1) * P],
                              banks[k % 3][:, 0:P]).then_inc(table_col, 1)
            dve.wait_ge(ends_landed, 16)
            dve.wait_ge(consts_ready, N_CONST)
            link(v.tensor_scalar(tmp_m[:NT], ends_bc[:NT, 0, :], thr[:NT], BIG, ALU.is_lt, ALU.mult))
            link(v.tensor_tensor(tmp_m[:NT], tmp_m[:NT], iota_m[:NT], ALU.add))
            v.tensor_reduce(lohi[:NT, 0:1], tmp_m[:NT], AX_X, ALU.min)
            link(v.tensor_scalar(lohi[:NT, 3:4], thr[:NT], float(P - 1), None, ALU.add))
            link(v.tensor_scalar(tmp_m[:NT], ends_bc[:NT, 1, :], lohi[:NT, 3:4], None, ALU.is_le))
            link(v.scalar_tensor_tensor(tmp_m[:NT], iota_m[:NT], 1.0, tmp_m[:NT], ALU.add, ALU.mult))
            v.tensor_scalar(lohi_i[:NT, 0:1], lohi[:NT, 0:1], float(ET), None, ALU.min)
            v.tensor_scalar(lohi_i[:NT, 1:2], lohi[:NT, 0:1], float(ET), float(SLOTS), ALU.min, ALU.add)
            link(v.tensor_reduce(lohi[:NT, 2:3], tmp_m[:NT], AX_X, ALU.max))
            v.tensor_scalar(lohi_i[:NT, 2:3], lohi[:NT, 0:1], float(ET), float(SLOTS + 1), ALU.min, ALU.add)
            v.tensor_copy(lohi_i[:NT, 3:4], lohi[:NT, 2:3]).then_inc(bounds_ready, 1)
            link.close()

        def tables_tensor(pe):
            pe.wait_ge(consts_ready, N_CONST)
            pe.wait_ge(ends_ready, 1)
            for k in range(2):
                nc.tensor.transpose(banks[k][0:EC, 0:P], ends[:, k, :], ident[:, :]).then_inc(ends_turned, 1)
            for k in range(3 * EC):
                if k < 2:
                    pe.wait_ge(ends_out, k + 1)
                if k >= 3:
                    pe.wait_ge(table_col, k - 2)
                nc.tensor.transpose(banks[k % 3][:, 0:P], rows[:, k // EC, k % EC, :], ident[:, :]
                                    ).then_inc(row_turned, 1)

        def load_ln_exp(act):
            act.add_instruction(mybir.InstLoadActFuncSet(name=nc.get_next_instruction_name(), act_func_set_id=6,
                                                         engine=mybir.EngineType.Activation, ins=[], outs=[]))

        xb = [view(work, 1792 * h, G, D) for h in range(2)]
        hb = [view(work, 3584 + 1792 * h, G, D) for h in range(2)]
        st = [view(work, 7168 + 200 * h, 200) for h in range(2)]
        x_landed = [sem(f"x_landed{h}") for h in range(2)]
        xlast_clear, s0_ready = sem("xlast_clear"), sem("s0_ready")
        xn_ready, xn_stored = sem("xn_ready"), [sem(f"xn_stored{h}") for h in range(2)]
        ln_in, ln_out, h0_ready = sem("ln_in"), sem("ln_out"), sem("h0_ready")
        h0_turned, h0T_ready, gram_used = sem("h0_turned"), sem("h0T_ready"), sem("gram_used")
        gram_done = sem("gram_done")
        norm_link = sem("norm_link")
        NG = NT // G
        qkv_flat = qkv[:, :, :, :, :].rearrange("p a b c d -> p a (b c d)")
        turn_bank = [banks[0][:, 0:D], banks[1][:, 0:D], banks[2][:, 0:D], banks[3][:, 0:D],
                     qkv_flat[:, 0, 0:D], qkv_flat[:, 1, 0:D], qkv_flat[:, 2, 0:D]]
        gram = banks[4]
        NORM_LINKS = 9
        var_ready, rsqrt_seed = sem("var_ready"), sem("rsqrt_seed")
        act_norm_link = sem("act_norm_link")

        def norm_cols(h):
            pair = [view(st[h], 56 + 16 * q, 2, 8)[:, :, 0:G] for q in range(3)]
            return pair + [st[h][:, 104 + 8 * q:104 + 8 * q + G] for q in range(4)]

        def newton(v, link, y, x_, t):
            link(v.tensor_tensor(t, y, y, ALU.mult))
            link(v.scalar_tensor_tensor(t, t, -0.5, x_, ALU.mult, ALU.mult))
            link(v.scalar_tensor_tensor(y, t, 1.5, y, ALU.add, ALU.mult))

        def node_rows(t, first, n):
            if isinstance(first, int):
                r = t[first * P:(first + n) * P, :]
            else:
                r = t[bass.ds(first * P, n * P), :]
            return r.rearrange("(t p) d -> p t d", p=P)

        def norm_sync(sp):
            def load(g, h):
                sp.dma_start(xb[h], node_rows(x, g * G, G)).then_inc(x_landed[h], 16)

            def store(g, h):
                sp.wait_ge(xn_ready, g + 1)
                sp.dma_start(node_rows(xn_dram, g * G, G), xb[h]).then_inc(xn_stored[h], 16)

            load(0, 0)
            load(1, 1)
            with sp.Fori(0, NG // 2 - 2) as u:
                for h in range(2):
                    store(u * 2 + h, h)
                sp.wait_ge(h0_ready, u * (2 * G) + 2 * G)
                for h in range(2):
                    sp.wait_ge(xn_stored[h], u * 16 + 16)
                    load(u * 2 + (h + 2), h)
            for h in range(2):
                store(NG - 4 + h, h)
            sp.wait_ge(xn_stored[0], 16 * (NG // 2 - 1))
            sp.wait_ge(h0_ready, (NG - 3) * G)
            load(NG - 2, 0)
            sp.wait_ge(xn_stored[1], 16 * (NG // 2 - 1))
            sp.wait_ge(h0_ready, (NG - 2) * G)
            sp.dma_start(xb[1][:, 0:G - 1], node_rows(x, (NG - 1) * G, G - 1)).then_inc(x_landed[1], 16)
            sp.wait_ge(xlast_clear, 1)
            sp.dma_start(xb[1][0:LAST, G - 1], x[(NT - 1) * P:N, :]).then_inc(x_landed[1], 16)
            store(NG - 2, 0)
            store(NG - 1, 1)

        stats_ready = sem("stats_ready")

        def norm_vector(dve, stats_turn):
            v = nc.vector
            def step(g, h, landed):
                link = Link(dve, norm_link, NORM_LINKS, g)
                stats = view(st[h], 0, G, 6)
                mv = view(st[h], 42, G, 2)
                var, y, t, num, den, ln, s0 = norm_cols(h)
                dve.wait_ge(x_landed[h], landed)
                for k in range(G - 1):
                    v.bn_stats(stats[:, k], xb[h][:, k])
                v.bn_stats(stats[:, G - 1], xb[h][:, G - 1]).then_inc(stats_ready, 1)
                if isinstance(g, int):
                    dve.wait_ge(stats_ready, g + 1)
                else:
                    counted(dve, stats_ready, stats_turn)
                for k in range(G - 1):
                    v.bn_aggr(mv[:, k], stats[:, k])
                link(v.bn_aggr(mv[:, G - 1], stats[:, G - 1]))
                v.tensor_scalar(var[:, 0], mv[:, :, 1], LN_EPS, None, ALU.add)
                v.tensor_scalar(var[:, 1], mv[:, :, 1], TINY, None, ALU.add).then_inc(var_ready, 1)
                dve.wait_ge(rsqrt_seed, g + 1)
                newton(v, link, y, var, t)
                for k in range(G):
                    ins = v.tensor_scalar(xb[h][:, k], xb[h][:, k], mv[:, k, 0:1], y[:, 0, k:k + 1],
                                          ALU.subtract, ALU.mult)
                ins.then_inc(xn_ready, 1)
                v.tensor_tensor(t[:, 0], var[:, 1], y[:, 1], ALU.mult)
                link(v.tensor_tensor(t[:, 1], var[:, 0], y[:, 0], ALU.mult))
                v.scalar_tensor_tensor(num, t[:, 0], float(D) ** 0.5, y[:, 0], ALU.mult, ALU.mult)
                link(v.scalar_tensor_tensor(s0, t[:, 1], float(D) ** -0.5, y[:, 1], ALU.mult, ALU.mult))
                link(v.tensor_scalar(num, num, 1e-15, BALL, ALU.max, ALU.min))
                link(v.tensor_scalar(den, num, -1.0, 1.0, ALU.mult, ALU.add))
                link(v.reciprocal(den, den))
                v.scalar_tensor_tensor(num, num, 1.0, den, ALU.add, ALU.mult).then_inc(ln_in, 1)
                dve.wait_ge(ln_out, g + 1)
                v.scalar_tensor_tensor(s0, ln, 0.5, s0, ALU.mult, ALU.mult).then_inc(s0_ready, 1)
                link.close()

            with dve.Fori(0, NG // 2 - 1) as u:
                step(u * 2, 0, u * 16 + 16)
                step(u * 2 + 1, 1, u * 16 + 16)
            dve.wait_ge(xn_stored[1], 16 * (NG // 2 - 1))
            dve.wait_ge(h0_ready, (NG - 2) * G)
            v.memset(xb[1][:, G - 1], 0.0).then_inc(xlast_clear, 1)
            step(NG - 2, 0, 16 * (NG // 2))
            step(NG - 1, 1, 16 * (NG // 2 + 1))

        def norm_scalar(act):
            turned = act.alloc_register("turned")
            act.reg_mov(turned, 1)
            load_ln_exp(act)

            def step(g, h, used):
                var, y, t, num, den, ln, s0 = norm_cols(h)
                link = Link(act, act_norm_link, 1, g)
                act.wait_ge(var_ready, g + 1)
                link(nc.scalar.activation(t, var, ACT.Ln))
                nc.scalar.activation(y, t, ACT.Exp, scale=-0.5).then_inc(rsqrt_seed, 1)
                link.close()
                act.wait_ge(ln_in, g + 1)
                nc.scalar.activation(ln, num, ACT.Ln).then_inc(ln_out, 1)
                act.wait_ge(s0_ready, g + 1)
                if used is not None:
                    act.wait_ge(gram_used, used)
                for k in range(G):
                    nc.scalar.activation(hb[h][:, k], xb[h][:, k], ACT.Copy, scale=s0[:, k:k + 1]
                                         ).then_inc(h0_ready, 1)
                for k in range(G):
                    counted(act, h0_turned, turned)
                    for c in range(C):
                        ins = nc.scalar.activation(h0T[:, c, bass.ds((g * G + k) * P, P)],
                                                   turn_bank[k][:, c * P:(c + 1) * P],
                                                   ACT.Copy, accum_out=h0_sums[:, c, bass.ds(g * G + k, 1)])
                    ins.then_inc(h0T_ready, 1)

            step(0, 0, None)
            step(1, 1, None)
            with act.Fori(1, NG // 2) as u:
                for h in range(2):
                    step(u * 2 + h, h, u * (2 * G) + (h - 1) * G)

        def norm_tensor(pe):
            for b in range(4):
                nc.tensor.matmul(gram[:, b * P:(b + 1) * P], zeros[:, :], zeros[:, :], start=(b == 0), stop=False,
                                 skip_group_check=True)

            def step(g, h, first):
                for k in range(G):
                    pe.wait_ge(h0_ready, g * G + (k + 1))
                    if not first:
                        pe.wait_ge(h0T_ready, g * G + (k + 1 - G))
                    for c in range(C):
                        ins = nc.tensor.transpose(turn_bank[k][:, c * P:(c + 1) * P], hb[h][:, k, c * P:(c + 1) * P],
                                                  ident[:, :])
                    ins.then_inc(h0_turned, 1)
                    for c in range(C):
                        ins = nc.tensor.matmul(gram[:, c * D:(c + 1) * D], hb[h][:, k, c * P:(c + 1) * P], hb[h][:, k],
                                               start=False, stop=False, skip_group_check=True)
                    ins.then_inc(gram_used, 1)

            step(0, 0, True)
            step(1, 1, False)
            with pe.Fori(1, NG // 2) as u:
                step(u * 2, 0, False)
                step(u * 2 + 1, 1, False)
            nc.tensor.matmul(gram[:, 0:P], zeros[:, :], zeros[:, :], start=False, stop=True,
                             skip_group_check=True).then_inc(gram_done, 1)

        gsb = view(work, 0, C, D)
        gw = view(work, 512, C, QC * P)
        bn_t = view(work, 2048 + 64, 64)
        gram_read, gw_done, gw_read, stat_done, bn_ready = (
            sem("gram_read"), sem("gw_done"), sem("gw_read"), sem("stat_done"), sem("bn_ready"))
        bn_link, bn_var_ready, bn_seed = sem("bn_link"), sem("bn_var_ready"), sem("bn_seed")
        bn_y = bn_t[:, 32:38]

        def bn_scalar(act):
            link = Link(act, act_bn_link, 1, 0)
            act.wait_ge(bn_var_ready, 1)
            link(nc.scalar.activation(bn_t[:, 40:46], bn_t[:, 16:22], ACT.Ln))
            nc.scalar.activation(bn_y, bn_t[:, 40:46], ACT.Exp, scale=-0.5).then_inc(bn_seed, 1)

        act_bn_link = sem("act_bn_link")
        gw_banks = [[banks[0][:, :], banks[1][:, 0:D]], [banks[2][:, :], banks[3][:, 0:D]]]

        def bn_vector(dve):
            v = nc.vector
            link = Link(dve, bn_link, 10, 0)
            mean, hm, t1, t2 = bn_t[:, 0:2], bn_t[:, 8:14], bn_t[:, 16:22], bn_t[:, 24:30]
            for h in range(2):
                dve.wait_ge(xn_stored[h], 16 * (NG // 2))
            dve.wait_ge(h0T_ready, NT)
            dve.wait_ge(gram_used, NT)
            link(v.tensor_reduce(mean, h0_sums[:, :, :], AX_X, ALU.add))
            v.tensor_scalar(mean, mean, 1.0 / N, None, ALU.mult)
            dve.wait_ge(gram_done, 1)
            v.tensor_scalar(gsb[:, :, :], gram.rearrange("p (c d) -> p c d", c=C), 1.0 / N, None, ALU.mult
                            ).then_inc(gram_read, 1)
            dve.wait_ge(params_landed, 16 * n_params)
            for q in range(QC):
                v.tensor_scalar(mixW[:, q, :], mixW[:, q, :], wdw[:, q:q + 1], None, ALU.mult)
            v.tensor_scalar(eps1_col, eps_col, 1.0, None, ALU.add)
            dve.wait_ge(gw_done, 1)
            for c in range(C):
                v.tensor_tensor(gw[:, c, 0:512], gw_banks[c][0], wqkvT[:, c, 0:512], ALU.mult)
                ins = v.tensor_tensor(gw[:, c, 512:768], gw_banks[c][1], wqkvT[:, c, 512:768], ALU.mult)
            ins.then_inc(gw_read, 1)
            dve.wait_ge(stat_done, 1)
            link(v.tensor_copy(hm, banks[4][:, 8:8 + QC]))
            link(v.tensor_tensor(t1, hm, hm, ALU.mult))
            link(v.tensor_tensor(t1, banks[4][:, 0:QC], t1, ALU.subtract))
            link(v.tensor_scalar(t1, t1, 0.0, LN_EPS, ALU.max, ALU.add))
            v.tensor_copy(t1, t1).then_inc(bn_var_ready, 1)
            dve.wait_ge(bn_seed, 1)
            newton(v, link, bn_y, t1, t2)
            link(v.tensor_tensor(bn_a, bn_y, gam, ALU.mult))
            link(v.tensor_tensor(t2, hm, bn_a, ALU.mult))
            v.tensor_tensor(bn_b, bet, t2, ALU.subtract).then_inc(bn_ready, 1)
            link.close()

        def bn_tensor(pe):
            pe.wait_ge(gram_read, 1)
            pe.wait_ge(params_landed, 16 * n_params)
            pe.wait_ge(h0T_ready, NT)
            for c in range(C):
                for part, (o, n) in enumerate(((0, 512), (512, 256))):
                    for b in range(C):
                        ins = nc.tensor.matmul(gw_banks[c][part], gsb[:, b, c * P:(c + 1) * P], wqkvT[:, b, o:o + n],
                                               start=(b == 0), stop=(b == C - 1))
            ins.then_inc(gw_done, 1)
            pe.wait_ge(gw_read, 1)
            for q in range(QC):
                for c in range(C):
                    nc.tensor.matmul(banks[4][:, q:q + 1], gw[:, c, q * P:(q + 1) * P], ones[:, 0:1],
                                     start=(c == 0), stop=(c == C - 1))
                for c in range(C):
                    ins = nc.tensor.matmul(banks[4][:, 8 + q:9 + q], wqkvT[:, c, q * P:(q + 1) * P],
                                           bn_t[:, c:c + 1], start=(c == 0), stop=(c == C - 1))
            ins.then_inc(stat_done, 1)

        xin = [view(work, D * h, D) for h in range(2)]
        xnin = [view(work, 512 + D * h, D) for h in range(2)]
        h2T = view(work, 1024, QC, 2 * P)
        rk = view(work, 2560, 512)
        vs = view(work, 3072, 512)
        ratio = view(work, 3584, 512)
        om = view(work, 4096, 512)
        outT = view(work, 4608, 4, P)
        ft = [view(work, 5120 + D * h, D) for h in range(2)]
        sup = [view(work, 5632 + D * h, D) for h in range(2)]
        supT = view(work, 6144, C, 2 * P)
        gT = view(work, 6656, C, 2 * P)
        u_row = view(work, 7168, D)
        x2b = [view(work, 7424 + D * h, D) for h in range(2)]
        pair = [view(work, 7936, 2, D), view(work, 10176, 2, D)]
        sq_ts = [view(work, 8448, QC, P), view(work, 9408, QC, P)]
        sq_om = view(work, 8448, 512)
        sq_ft = [view(work, 9408 + D * h, D) for h in range(2)]
        mix_s = [view(work, 9216 + 64 * h, 64) for h in range(2)]
        nsq = [m[:, 0:2] for m in mix_s]
        n3sq = [m[:, 2:3] for m in mix_s]
        s_col = [m[:, 4:5] for m in mix_s]
        c_col = [m[:, 5:6] for m in mix_s]
        s_y = [m[:, 6:8] for m in mix_s]
        s_t = [m[:, 8:10] for m in mix_s]
        n3_y = [m[:, 10:11] for m in mix_s]
        n3_t = [m[:, 11:12] for m in mix_s]
        pair_s = view(work, 9344, 64)
        n4sq, n4_y, n4_t, n4, e4, f4 = (pair_s[:, 2 * q:2 * q + 2] for q in range(6))
        tail_mv = view(pair_s, 16, 2, 2)
        tail_var, tail_y, tail_t, tail_acc = (pair_s[:, 20 + 2 * q:22 + 2 * q] for q in range(4))
        f_col = [f4[:, h:h + 1] for h in range(2)]
        tail_stats = [pair_s[:, 32 + 6 * h:38 + 6 * h] for h in range(2)]
        sumk = [m[:, 16:32] for m in mix_s]

        slot_used = sem("slot_used")
        msg_landed = [sem(f"msg_landed{q}") for q in range(RING)]
        sel_ready, staged, agg_done = sem("sel_ready"), sem("staged"), sem("agg_done")
        rem_used, rem_ready, rem_landed = sem("rem_used"), sem("rem_ready"), sem("rem_landed")
        iota_ready = sem("iota_ready")
        h1_done, h2_ready, s2_done, nsq_ready, s_ready = (
            sem("h1_done"), sem("h2_ready"), sem("s2_done"), sem("nsq_ready"), sem("s_ready"))
        vs_ready, v_read, om_ready, n3_ready = sem("vs_ready"), sem("v_read"), sem("om_ready"), sem("n3_ready")
        om_turned, outT_ready, ft_done, ft_read = (
            sem("om_turned"), sem("outT_ready"), sem("ft_done"), sem("ft_read"))
        n4_ready, n4c_ready, th_ready = sem("n4_ready"), sem("n4c_ready"), sem("th_ready")
        tot_ready, s_seed, var2_ready, var2_seed = sem("tot_ready"), sem("s_seed"), sem("var2_ready"), sem("var2_seed")
        act_mix_link, act_tail_link = sem("act_mix_link"), sem("act_tail_link")
        sup_ready, sup_turned, supT_ready = sem("sup_ready"), sem("sup_turned"), sem("supT_ready")
        w1_done, g1_ready, w2_done, w2_read = sem("w1_done"), sem("g1_ready"), sem("w2_done"), sem("w2_read")
        out_ready = sem("out_ready")
        xin_landed = [sem(f"xin_landed{h}") for h in range(2)]
        xnin_landed = [sem(f"xnin_landed{h}") for h in range(2)]
        pair_stored = [sem(f"pair_stored{h}") for h in range(2)]
        base_stored = [sem(f"base_stored{h}") for h in range(2)]
        mix_link, tail_link = sem("mix_link"), sem("tail_link")

        def after(eng, s, v):
            if not (isinstance(v, int) and v <= 0):
                eng.wait_ge(s, v)

        def row_range(t, first, n):
            return t[bass.ds(first, n), :] if not isinstance(first, int) else t[first:first + n, :]

        def remainder(eng, t, first, body):
            lo = eng.value_load(bounds[0:1, bass.ds(t * 4 + 1, 1)], min_val=0, max_val=ET + SLOTS)
            hi = eng.value_load(bounds[0:1, bass.ds(t * 4 + 3, 1)], min_val=0, max_val=ET)
            with eng.If(lo < hi):
                first(lo)
                lo1 = eng.value_load(bounds[0:1, bass.ds(t * 4 + 2, 1)], min_val=0, max_val=ET + SLOTS + 1)
                with eng.If(lo1 < hi):
                    with eng.Fori(lo1, hi) as m:
                        body(m)

        def main_sync(sp):
            def load_xn(i, h):
                after(sp, sup_ready, i * 2 + (h - 1))
                sp.dma_start(xnin[h], row_range(xn_dram, i * (2 * P) + h * P, P)).then_inc(xnin_landed[h], 16)

            def load_x(j, h, n=P):
                after(sp, out_ready, j * 2)
                sp.dma_start(xin[h][:n], row_range(x, j * (2 * P) + h * P, n)).then_inc(xin_landed[h], 16)

            def store(j, h, n=P):
                sp.wait_ge(out_ready, j * 2 + (h + 1))
                sp.dma_start(row_range(pair_dram, j * (2 * P) + h * P, P), pair[h].rearrange("p a d -> p (a d)")
                             ).then_inc(pair_stored[h], 16)
                sp.dma_start(row_range(out, j * (2 * P) + h * P, n), pair[h][:n, 0]).then_inc(base_stored[h], 16)

            sp.wait_ge(bn_ready, 1)
            load_xn(0, 0)
            load_xn(0, 1)

            def step(i):
                load_xn(i, 0)
                load_x(i - 1, 0)
                load_xn(i, 1)
                load_x(i - 1, 1)
                store(i - 1, 0)
                store(i - 1, 1)

            step(1)
            with sp.Fori(2, NS) as i:
                step(i)
            load_x(NS - 1, 0)
            load_x(NS - 1, 1, LAST)
            store(NS - 1, 0)
            store(NS - 1, 1, LAST)

        def main_pool(pool):
            pool.wait_ge(table_col, 3 * EC)
            pool.wait_ge(bounds_landed, 16)
            for h in range(2):
                pool.wait_ge(xn_stored[h], 16 * (NG // 2))
            turn, rem = pool.alloc_register("turn_p"), pool.alloc_register("rem_p")
            stage = pool.alloc_register("stage_p")
            pool.reg_mov(stage, 1)
            pool.reg_mov(turn, 1)
            pool.reg_mov(rem, 1)

            def rem_body(m):
                counted(pool, rem_ready, rem)
                nc.gpsimd.indirect_dma_start(out=rem_msg[:, :], out_offset=None, in_=xn_dram[:, :],
                                             in_offset=bass.IndirectOffsetOnAxis(ap=rem_src[:, :], axis=0)
                                             ).then_inc(rem_landed, 16)

            def rem_first(h):
                def first(m):
                    counted(pool, rem_used, rem)
                    nc.gpsimd.indirect_dma_start(
                        out=rem_msg[:, :], out_offset=None, in_=xn_dram[:, :],
                        in_offset=bass.IndirectOffsetOnAxis(ap=src_stage[h][:, SLOTS:SLOTS + 1], axis=0)
                    ).then_inc(rem_landed, 16)
                return first

            with pool.Fori(0, NS) as i:
                for h in range(2):
                    counted(pool, staged, stage)
                    for k in range(SLOTS):
                        q = (h * SLOTS + k) % RING
                        counted(pool, slot_used, turn)
                        nc.gpsimd.indirect_dma_start(
                            out=msg[q][:, :], out_offset=None, in_=xn_dram[:, :],
                            in_offset=bass.IndirectOffsetOnAxis(ap=src_stage[h][:, k:k + 1], axis=0)
                        ).then_inc(msg_landed[q], 16)
                    remainder(pool, i * 2 + h, rem_first(h), rem_body)

        def main_scalar(act):
            s = nc.scalar

            def mix_norms(i, h):
                act.wait_ge(s2_done, i * 2 + (h + 1))
                after(act, om_ready, i * 2 + h)
                s.activation(sq_ts[0], qkv[:, :, :, 0, :].rearrange("p r i c -> p (r i) c"),
                             ACT.Square, accum_out=nsq[h][:, 0:1])
                s.activation(sq_ts[1], qkv[:, :, :, 1, :].rearrange("p r i c -> p (r i) c"),
                             ACT.Square, accum_out=nsq[h][:, 1:2])
                s.activation(rk, qkv[:, 1].rearrange("p i s c -> p (i s c)"), ACT.Relu).then_inc(nsq_ready, 1)

            def mix_s_seed(i, h, link):
                act.wait_ge(tot_ready, i * 2 + (h + 1))
                link(s.activation(s_t[h], nsq[h], ACT.Ln))
                s.activation(s_y[h], s_t[h], ACT.Exp, scale=-0.5).then_inc(s_seed, 1)

            def mix_v(i, h):
                act.wait_ge(s_ready, i * 2 + (h + 1))
                s.activation(vs, qkv[:, 2].rearrange("p i s c -> p (i s c)"), ACT.Identity, scale=s_col[h],
                             bias=att_eps_col).then_inc(vs_ready, 1)

            def mix_n3(i, h, link):
                act.wait_ge(om_ready, i * 2 + (h + 1))
                link(s.activation(sq_om, om, ACT.Square, accum_out=n3sq[h]))
                link(s.activation(n3_t[h], n3sq[h], ACT.Ln, bias=tiny_col))
                s.activation(n3_y[h], n3_t[h], ACT.Exp, scale=-0.5).then_inc(n3_ready, 1)

            def mix_outT(i, h):
                act.wait_ge(om_turned, i * 2 + (h + 1))
                after(act, ft_done, i * 2 + h)
                s.activation(outT.rearrange("p c n -> p (c n)"), banks[2 if h == 0 else 1][:, :], ACT.Copy
                             ).then_inc(outT_ready, 1)

            def mix_n4(i, h):
                act.wait_ge(ft_read, i * 2 + (h + 1))
                return s.activation(sq_ft[h], ft[h], ACT.Square, accum_out=n4sq[:, h:h + 1])

            def mix_n4_seed(i, link):
                link(mix_n4(i, 1))
                link(s.activation(n4_t, n4sq, ACT.Ln, bias=tiny_col))
                s.activation(n4_y, n4_t, ACT.Exp, scale=-0.5).then_inc(n4_ready, 1)

            def mix_exp(i):
                act.wait_ge(n4c_ready, i + 1)
                s.activation(e4, n4, ACT.Exp, scale=-2.0).then_inc(th_ready, 1)

            def tail_var_seed(j, link):
                act.wait_ge(var2_ready, j + 1)
                link(s.activation(tail_t, tail_var, ACT.Ln))
                s.activation(tail_y, tail_t, ACT.Exp, scale=-0.5).then_inc(var2_seed, 1)

            def tail_supT(j, h):
                act.wait_ge(sup_turned, j * 2 + (h + 1))
                after(act, w1_done, j)
                s.activation(supT[:, :, h * P:(h + 1) * P], banks[h][:, 0:D].rearrange("p (c n) -> p c n", c=C),
                             ACT.Copy).then_inc(supT_ready, 1)

            def tail_g1(j):
                act.wait_ge(w1_done, j + 1)
                after(act, w2_done, j * 2)
                for c in range(C):
                    ins = s.activation(gT[:, c], banks[2][:, c * D:(c + 1) * D], ACT.Relu, bias=b1_col[:, c:c + 1])
                ins.then_inc(g1_ready, 1)

            def mix_h2(i):
                after(act, s2_done, i * 2)
                for q in range(3):
                    act.wait_ge(h1_done, i * 3 + (q + 1))
                    for e in range(2):
                        k = 2 * q + e
                        ins = s.activation(h2T[:, k], banks[q][:, e * D:(e + 1) * D], ACT.Relu,
                                           scale=bn_a[:, k:k + 1], bias=bn_b[:, k:k + 1])
                    ins.then_inc(h2_ready, 1)

            def step(i, j):
                mix = Link(act, act_mix_link, 6, i)
                tail = Link(act, act_tail_link, 3, j)
                if j is not None:
                    mix_n4_seed(j, tail)
                    mix_exp(j)
                if j is not None:
                    tail_supT(j, 0)
                    tail_supT(j, 1)
                mix_norms(i, 0)
                if j is not None:
                    tail_g1(j)
                mix_s_seed(i, 0, mix)
                mix_v(i, 0)
                mix_n3(i, 0, mix)
                mix_outT(i, 0)
                mix_norms(i, 1)
                if j is not None:
                    tail_var_seed(j, tail)
                    tail.close()
                mix_s_seed(i, 1, mix)
                mix_v(i, 1)
                mix_n4(i, 0)
                mix_n3(i, 1, mix)
                mix_outT(i, 1)
                mix.close()
                if not (isinstance(i, int) and i == NS - 1):
                    mix_h2(i + 1)

            act.wait_ge(bn_ready, 1)
            mix_h2(0)
            step(0, None)
            step(1, 0)
            with act.Fori(2, NS - 1) as i:
                step(i, i - 1)
            step(NS - 1, NS - 2)
            tail = Link(act, act_tail_link, 3, NS - 1)
            mix_n4_seed(NS - 1, tail)
            mix_exp(NS - 1)
            tail_supT(NS - 1, 0)
            tail_supT(NS - 1, 1)
            tail_g1(NS - 1)
            tail_var_seed(NS - 1, tail)
            tail.close()

        MIX_LINKS, TAIL_LINKS = 24, 20
        STAGE_AT = 2

        def main_vector(dve, stats_turn):
            v = nc.vector
            rem = dve.alloc_register("rem_v")
            dve.reg_mov(rem, 1)

            def one_hot(dst_ap, h, m):
                return v.tensor_scalar(dst_ap, iota_t[h][:, :], dstT[:, bass.ds(m, 1)], ewT[:, bass.ds(m, 1)],
                                       ALU.is_equal, ALU.mult)

            def first_tile(i, h):
                return dve.value_load(bounds[0:1, bass.ds(i * 8 + h * 4, 1)], min_val=0, max_val=ET)

            def start_tile(i, h):
                t = i * 2 + h
                lo = first_tile(i, h)
                after(dve, slot_used, i * STEP_SLOTS + (h * SLOTS - SLOTS + RING + 1))
                v.tensor_scalar(iota_t[h][:, :], iota[:, :], tile_col[:, bass.ds(t, 1)], None, ALU.add
                                ).then_inc(iota_ready, 1)
                v.tensor_scalar(src_stage[h][:, :], srcT[:, bass.ds(lo, SLOTS + 1)], 0.0, None, ALU.add
                                ).then_inc(staged, 1)

            def edge(i, k, lo):
                dve.wait_ge(slot_used, i * STEP_SLOTS + (k + 1))
                if k % SLOTS == 0:
                    dve.wait_ge(iota_ready, i * 2 + (k // SLOTS + 1))
                one_hot(sel[k % RING][:, :], k // SLOTS, lo + k % SLOTS).then_inc(sel_ready, 1)
                if k % SLOTS == SLOTS - 1:
                    rem_first(i, k // SLOTS)

            def rem_range(i, h, first):
                at = i * 8 + h * 4
                return (dve.value_load(bounds[0:1, bass.ds(at + first, 1)], min_val=0, max_val=ET + SLOTS + 1),
                        dve.value_load(bounds[0:1, bass.ds(at + 3, 1)], min_val=0, max_val=ET))

            def rem_first(i, h):
                lo, hi = rem_range(i, h, 1)
                with dve.If(lo < hi):
                    dve.wait_ge(rem_used, dve.snap(rem, min_val=1, max_val=1 << 20))
                    one_hot(rem_sel[:, :], h, lo).then_inc(rem_ready, 1)
                    dve.reg_add(rem, rem, 1)

            def rem_more(i, h):
                lo, hi = rem_range(i, h, 2)
                with dve.If(lo < hi):
                    with dve.Fori(lo, hi) as m:
                        dve.wait_ge(rem_used, dve.snap(rem, min_val=1, max_val=1 << 20))
                        v.tensor_scalar(rem_src[:, :], srcT[:, bass.ds(m, 1)], 0.0, None, ALU.add)
                        one_hot(rem_sel[:, :], h, m).then_inc(rem_ready, 1)
                        dve.reg_add(rem, rem, 1)

            def mix_norms(i, h, link):
                dve.wait_ge(nsq_ready, i * 2 + (h + 1))
                v.tensor_reduce(sumk[h], rk.rearrange("p (g d) -> p g d", d=32), AX_X, ALU.add)
                link(v.scalar_tensor_tensor(nsq[h][:, 1:2], nsq[h][:, 0:1], TINY, nsq[h][:, 1:2], ALU.add, ALU.add))
                v.tensor_scalar(nsq[h][:, 0:1], nsq[h][:, 0:1], TINY, None, ALU.add).then_inc(tot_ready, 1)

            def mix_scale(i, h, link):
                dve.wait_ge(s_seed, i * 2 + (h + 1))
                newton(v, link, s_y[h], nsq[h], s_t[h])
                link(v.tensor_scalar(s_y[h], s_y[h], AMAX, 1.0, ALU.mult, ALU.min))
                v.tensor_tensor(s_col[h], s_y[h][:, 0:1], s_y[h][:, 1:2], ALU.min).then_inc(s_ready, 1)

            def mix_out(i, h, link):
                dve.wait_ge(s_ready, i * 2 + (h + 1))
                dve.wait_ge(vs_ready, i * 2 + (h + 1))
                link(v.reciprocal(ratio, vs))
                link(v.scalar_tensor_tensor(ratio, qkv[:, 2].rearrange("p i s c -> p (i s c)"), s_col[h], ratio,
                                            ALU.mult, ALU.mult))
                after(dve, om_turned, i * 2 + h)
                after(dve, n3_ready, i * 2 + h)
                v.scalar_tensor_tensor(om, qkv[:, 0].rearrange("p i s c -> p (i s c)"), 0.0, ratio,
                                       ALU.max, ALU.mult).then_inc(v_read, 1)
                dve.wait_ge(v_read, i * 2 + (h + 1))
                v.tensor_tensor(om.rearrange("p (g d) -> p g d", d=32), om.rearrange("p (g d) -> p g d", d=32),
                                sumk[h].unsqueeze(2).broadcast_to([P, 16, 32]), ALU.mult).then_inc(om_ready, 1)

            def mix_c(i, h, link):
                dve.wait_ge(n3_ready, i * 2 + (h + 1))
                newton(v, link, n3_y[h], n3sq[h], n3_t[h])
                link(v.tensor_tensor(n3_t[h], s_col[h], s_col[h], ALU.mult))
                link(v.scalar_tensor_tensor(c_col[h], n3_y[h], AMAX, n3_t[h], ALU.mult, ALU.min))

            def mix_ft(i, h):
                dve.wait_ge(ft_done, i * 2 + (h + 1))
                v.scalar_tensor_tensor(ft[h], banks[0 if h == 0 else 2][:, 0:D], c_col[h], bres_row[:, :],
                                       ALU.mult, ALU.add).then_inc(ft_read, 1)

            def mix_n4(i, link):
                dve.wait_ge(n4_ready, i + 1)
                newton(v, link, n4_y, n4sq, n4_t)
                v.tensor_tensor(n4, n4sq, n4_y, ALU.mult).then_inc(n4c_ready, 1)

            def mix_f(i, link):
                dve.wait_ge(th_ready, i + 1)
                link(v.tensor_scalar(n4_t, e4, 1.0, None, ALU.add))
                v.tensor_scalar(e4, e4, -1.0, 1.0, ALU.mult, ALU.add)
                link(v.reciprocal(n4_t, n4_t))
                link(v.tensor_tensor(e4, e4, n4_t, ALU.mult))
                link(v.scalar_tensor_tensor(f4, e4, BALL, n4_y, ALU.min, ALU.mult))

            def take_sup(i, h):
                dve.wait_ge(agg_done, i * 2 + (h + 1))
                dve.wait_ge(xnin_landed[h], i * 16 + 16)
                after(dve, sup_turned, i * 2 + (h - 1))
                v.scalar_tensor_tensor(sup[h], xnin[h], eps1_col, agg[h][:, 0:D], ALU.mult, ALU.add
                                       ).then_inc(sup_ready, 1)

            def combine(j, h, link):
                dve.wait_ge(w2_done, j * 2 + (h + 1))
                dve.wait_ge(xin_landed[h], j * 16 + 16)
                v.tensor_tensor(u_row, xin[h], banks[h][:, 0:D], ALU.add).then_inc(w2_read, 1)
                dve.wait_ge(w2_read, j * 2 + (h + 1))
                link(v.tensor_tensor(u_row, u_row, b2_row[:, :], ALU.add))
                link(v.scalar_tensor_tensor(x2b[h], ft[h], f_col[h], u_row, ALU.mult, ALU.add))
                v.bn_stats(tail_stats[h], x2b[h]).then_inc(stats_ready, 1)
                if isinstance(j, int):
                    dve.wait_ge(stats_ready, NG + 2 * j + h + 1)
                else:
                    counted(dve, stats_ready, stats_turn)
                link(v.bn_aggr(tail_mv[:, h], tail_stats[h]))

            def tail_variance(j):
                v.tensor_scalar(tail_var, tail_mv[:, :, 1], LN_EPS, None, ALU.add).then_inc(var2_ready, 1)

            def tail_rstd(j, link):
                dve.wait_ge(var2_seed, j + 1)
                newton(v, link, tail_y, tail_var, tail_t)

            def tail_out(j, h, link):
                after(dve, pair_stored[h], j * 16)
                after(dve, base_stored[h], j * 16)
                link(v.tensor_scalar(pair[h][:, 1], x2b[h], tail_mv[:, h, 0:1], tail_y[:, h:h + 1], ALU.subtract, ALU.mult))
                v.tensor_tensor_reduce(u_row, pair[h][:, 1], wr_row[:, :], 1.0, 0.0, ALU.mult, ALU.add, tail_acc[:, h:h + 1])
                link(v.tensor_tensor(pair[h][:, 0], x2b[h], pair[h][:, 1], ALU.add))
                v.tensor_scalar(route_w[:, bass.ds(j * 2 + h, 1)], tail_acc[:, h:h + 1], br_col, None, ALU.add
                                ).then_inc(out_ready, 1)

            def step(i, j):
                mix = Link(dve, mix_link, MIX_LINKS, i)
                tail = Link(dve, tail_link, TAIL_LINKS, j)
                last = isinstance(i, int) and i == NS - 1
                lo = first_tile(i, 0)
                for k in range(STEP_SLOTS):
                    ahead = k + LEAD
                    nxt = ahead >= STEP_SLOTS
                    if ahead % SLOTS == 0 and not (last and nxt):
                        lo = first_tile(i + nxt, ahead // SLOTS % 2)
                    if not (last and nxt):
                        edge(i + nxt, ahead % STEP_SLOTS, lo)
                    if k == STAGE_AT:
                        start_tile(i, 1)
                    if k == SLOTS + STAGE_AT and not last:
                        start_tile(i + 1, 0)
                    if j is not None:
                        if k == 0:
                            take_sup(j, 1)
                        if k == 2:
                            mix_n4(j, tail)
                        if k == 4:
                            mix_f(j, tail)
                        if k == 12:
                            combine(j, 0, tail)
                        if k == 13:
                            combine(j, 1, tail)
                            tail_variance(j)
                        if k == 22:
                            tail_rstd(j, tail)
                            tail_out(j, 0, tail)
                        if k == 24:
                            tail_out(j, 1, tail)
                            tail.close()
                    for h, (norms_at, scale_at, out_at, c_at, ft_at) in ((0, (5, 7, 9, 14, 17)),
                                                                         (1, (16, 19, 20, 24, 30))):
                        if k == norms_at:
                            mix_norms(i, h, mix)
                        if k == scale_at:
                            mix_scale(i, h, mix)
                        if k == out_at:
                            mix_out(i, h, mix)
                        if k == c_at:
                            mix_c(i, h, mix)
                        if k == ft_at:
                            mix_ft(i, h)
                    if k == SLOTS:
                        take_sup(i, 0)
                    if k % SLOTS == SLOTS - 1:
                        rem_more(i, k // SLOTS)
                mix.close()

            start_tile(0, 0)
            lo = first_tile(0, 0)
            for k in range(LEAD):
                edge(0, k, lo)
            step(0, None)
            step(1, 0)
            dve.reg_mov(stats_turn, NG + 3)
            with dve.Fori(2, NS - 1) as i:
                step(i, i - 1)
            step(NS - 1, NS - 2)
            take_sup(NS - 1, 1)
            tail = Link(dve, tail_link, TAIL_LINKS, NS - 1)
            mix_n4(NS - 1, tail)
            mix_f(NS - 1, tail)
            combine(NS - 1, 0, tail)
            combine(NS - 1, 1, tail)
            tail_variance(NS - 1)
            tail_rstd(NS - 1, tail)
            tail_out(NS - 1, 0, tail)
            tail_out(NS - 1, 1, tail)
            tail.close()

        def main_tensor(pe):
            te = nc.tensor
            rem = pe.alloc_register("rem_t")
            pe.reg_mov(rem, 1)

            def edge(i, k):
                h, q = k // SLOTS, k % RING
                if k % SLOTS == 0:
                    after(pe, sup_ready, i * 2 + (h - 1))
                pe.wait_ge(sel_ready, i * STEP_SLOTS + (k + 1))
                pe.wait_ge(msg_landed[q], i * (16 * TURNS) + 16 * (k // RING + 1))
                te.matmul(agg[h][:, 0:D], sel[q][:, :], msg[q][:, :], start=(k % SLOTS == 0), stop=False,
                          skip_group_check=True).then_inc(slot_used, 1)

            def end_tile(i, h):
                def body(m):
                    r = pe.snap(rem, min_val=1, max_val=1 << 20)
                    pe.wait_ge(rem_ready, r)
                    pe.wait_ge(rem_landed, r * 16)
                    te.matmul(agg[h][:, 0:D], rem_sel[:, :], rem_msg[:, :], start=False, stop=False,
                              skip_group_check=True).then_inc(rem_used, 1)
                    pe.reg_add(rem, rem, 1)
                remainder(pe, i * 2 + h, body, body)
                te.matmul(agg[h][:, 0:1], zeros[:, :], zeros[:, 0:1], start=False, stop=True,
                          skip_group_check=True).then_inc(agg_done, 1)

            def mix_h1(i, q):
                after(pe, ft_read if q != 1 else outT_ready, i * 2 - (1 if q == 0 else 0))
                for e in range(2):
                    k = 2 * q + e
                    for c in range(C):
                        ins = te.matmul(banks[q][:, e * D:(e + 1) * D], wqkvT[:, c, k * P:(k + 1) * P],
                                        h0T[:, c, bass.ds(i * (2 * P), 2 * P)], start=(c == 0), stop=(c == C - 1))
                ins.then_inc(h1_done, 1)

            def mix_qkv(i, h):
                pe.wait_ge(h2_ready, i * 3 + 3)
                after(pe, v_read, i * 2 + h)
                for k in range(QC):
                    lhs = h2T[:, k, h * P:(h + 1) * P]
                    te.transpose(qkv[:, k // 2, k % 2, 0, :], lhs, ident[:, :])
                    ins = te.matmul(qkv[:, k // 2, k % 2, 1, :], lhs, mixW[:, k, :], start=True, stop=True)
                ins.then_inc(s2_done, 1)

            def mix_outT(i, j, h):
                pe.wait_ge(om_ready, i * 2 + (h + 1))
                if h == 0 and j is not None:
                    pe.wait_ge(g1_ready, j + 1)
                if h == 1 and j is not None:
                    pe.wait_ge(w2_read, j * 2 + 2)
                for c in range(4):
                    ins = te.transpose(banks[2 if h == 0 else 1][:, c * P:(c + 1) * P], om[:, c * P:(c + 1) * P],
                                       ident[:, :])
                ins.then_inc(om_turned, 1)

            def mix_ft(i, j, h):
                pe.wait_ge(outT_ready, i * 2 + (h + 1))
                if h == 0 and j is not None:
                    pe.wait_ge(w2_read, j * 2 + 1)
                for c in range(4):
                    ins = te.matmul(banks[0 if h == 0 else 2][:, 0:D], outT[:, c], wresT[:, c],
                                    start=(c == 0), stop=(c == 3))
                ins.then_inc(ft_done, 1)

            def tail_supT(j, h):
                pe.wait_ge(sup_ready, j * 2 + (h + 1))
                if isinstance(j, int) and j == NS - 1:
                    pe.wait_ge(ft_read, 2 * NS)
                    pe.wait_ge(outT_ready, 2 * NS)
                else:
                    pe.wait_ge(h2_ready, j * 3 + (4 + h))
                for c in range(C):
                    ins = te.transpose(banks[h][:, c * P:(c + 1) * P], sup[h][:, c * P:(c + 1) * P], ident[:, :])
                ins.then_inc(sup_turned, 1)

            def tail_w1(j):
                pe.wait_ge(supT_ready, j * 2 + 2)
                if not (isinstance(j, int) and j == NS - 1):
                    pe.wait_ge(h2_ready, j * 3 + 6)
                for m in range(C):
                    for c in range(C):
                        ins = te.matmul(banks[2][:, m * D:(m + 1) * D], w1T[:, c, m * P:(m + 1) * P], supT[:, c],
                                        start=(c == 0), stop=(c == C - 1))
                ins.then_inc(w1_done, 1)

            def tail_w2(j, h):
                pe.wait_ge(g1_ready, j + 1)
                for c in range(C):
                    ins = te.matmul(banks[h][:, 0:D], gT[:, c, h * P:(h + 1) * P], w2T[:, c],
                                    start=(c == 0), stop=(c == C - 1))
                ins.then_inc(w2_done, 1)

            def step(i, j):
                for k in range(STEP_SLOTS):
                    edge(i, k)
                    if k % SLOTS == SLOTS - 1:
                        end_tile(i, k // SLOTS)
                    if j is not None:
                        if k in (1, 3):
                            tail_supT(j, k // 2)
                        if k == 5:
                            tail_w1(j)
                        if k in (8, 9):
                            tail_w2(j, k - 8)
                    if k == 2:
                        mix_qkv(i, 0)
                    if k == 15:
                        mix_qkv(i, 1)
                    if k == 14:
                        mix_outT(i, j, 0)
                    if k == 17:
                        mix_ft(i, j, 0)
                    if k == 25:
                        mix_outT(i, j, 1)
                    if k == 28:
                        mix_ft(i, j, 1)
                    if k in (32, 33, 35) and not (isinstance(i, int) and i == NS - 1):
                        mix_h1(i + 1, (k - 31) // 2)

            pe.wait_ge(bn_ready, 1)
            te.matmul(agg[0][:, 0:1], zeros[:, :], zeros[:, 0:1], start=True, stop=True).then_inc(slot_used, RING)
            te.matmul(agg[0][:, 0:1], zeros[:, :], zeros[:, 0:1], start=True, stop=True).then_inc(rem_used, 1)
            for q in range(3):
                mix_h1(0, q)
            step(0, None)
            step(1, 0)
            with pe.Fori(2, NS - 1) as i:
                step(i, i - 1)
            step(NS - 1, NS - 2)
            tail_supT(NS - 1, 0)
            tail_supT(NS - 1, 1)
            tail_w1(NS - 1)
            tail_w2(NS - 1, 0)
            tail_w2(NS - 1, 1)

        BITS = 31
        at = lambda n, w: resident[:, n:n + w]
        wm, vv, flag, gt, eq, pre, incl, selm = (at(100 * q, NT) for q in range(8))
        rank_i, r_i, q_i = (at(800 + 100 * q, NT).bitcast(I32) for q in range(3))
        r_f, q_f, tok = (at(1100 + 100 * q, NT) for q in range(3))
        bits = at(1400, BITS).bitcast(I32)
        bits_f = at(1460, BITS)
        col = [at(1440 + q, 1) for q in range(12)]
        cnt, cge, sgn, kcol, thresh, need, part = col[:7]
        m_i, cand_i, inc_i = (c.bitcast(I32) for c in col[7:10])
        p_col = col[10]
        hot_r = [at(1500 + 128 * q, P) for q in range(2)]
        hot_q = [at(1760 + 64 * q, QW) for q in range(2)]
        ids = at(1900, QW).bitcast(I32)
        route_free, route_consts, wm_ready, v_scaled, vv_ready = (
            sem("route_free"), sem("route_consts"), sem("wm_ready"), sem("v_scaled"), sem("vv_ready"))
        cnt_ready, tot_done, bit_link, route_link = sem("cnt_ready"), sem("tot_done"), sem("bit_link"), sem("route_link")
        mask_ready, prefix_done, sel_set, prefix2_done = (
            sem("mask_ready"), sem("prefix_done"), sem("sel_set"), sem("prefix2_done"))
        hot_ready, hot_used, ids_done, ids_ready = sem("hot_ready"), sem("hot_used"), sem("ids_done"), sem("ids_ready")

        def only_nodes(pool, dst_ap, src_ap):
            return nc.gpsimd.affine_select(out=dst_ap, in_=src_ap, compare_op=ALU.is_ge, fill=LOWEST, base=N - 1,
                                           pattern=[[-P, NT]], channel_multiplier=-1)

        def route_pool(pool):
            pool.wait_ge(h1_done, 3 * NS)
            for b in range(BITS):
                nc.gpsimd.memset(bits[:, b:b + 1], 1 << (BITS - 1 - b))
            nc.gpsimd.iota(p_col, [[0, 1]], base=0, channel_multiplier=1, allow_small_or_imprecise_dtypes=True
                           ).then_inc(route_consts, 1)
            pool.wait_ge(out_ready, 2 * NS)
            only_nodes(pool, wm, route_w[:, :]).then_inc(wm_ready, 1)
            pool.wait_ge(v_scaled, 1)
            only_nodes(pool, vv, vv).then_inc(vv_ready, 1)

        def ranks(v, link, counts):
            link(v.tensor_copy(pre, counts[:, 0:NT]))
            link(v.tensor_tensor_scan(incl, ones[:, 0:NT], counts[:, P:P + NT], 0.0, ALU.mult, ALU.add))
            link(v.tensor_tensor(pre, pre, incl, ALU.add))
            link(v.tensor_tensor(pre, pre, counts[:, P:P + NT], ALU.subtract))

        def route_vector(dve):
            v = nc.vector
            link = Link(dve, route_link, 20, 0)
            dve.wait_ge(wm_ready, 1)
            dve.wait_ge(route_consts, 1)
            link(v.tensor_scalar(flag, wm, 0.0, None, ALU.is_ge))
            v.tensor_reduce(cnt, flag, AX_X, ALU.add).then_inc(cnt_ready, 1)
            v.memset(m_i, 0)
            v.tensor_copy(bits_f, bits)
            v.tensor_scalar(tok, tile_col[:, :], p_col, None, ALU.add)
            dve.wait_ge(tot_done, 1)
            link(v.tensor_scalar(cge, banks[0][:, 0:1], float(TOP), None, ALU.is_ge))
            v.tensor_scalar(kcol, cge, float(2 * TOP - N - 1), float(N - TOP + 1), ALU.mult, ALU.add)
            link(v.tensor_scalar(sgn, cge, 2.0, -1.0, ALU.mult, ALU.add))
            v.tensor_scalar(vv, wm, sgn, None, ALU.mult).then_inc(v_scaled, 1)
            dve.wait_ge(vv_ready, 1)
            with dve.Fori(0, BITS) as b:
                step = Link(dve, bit_link, 4, b)
                step(v.tensor_tensor(cand_i, m_i, bits[:, bass.ds(b, 1)], ALU.bitwise_or))
                step(v.tensor_scalar(flag, vv, cand_i.bitcast(F32), None, ALU.is_ge))
                v.tensor_reduce(cnt, flag, AX_X, ALU.add).then_inc(cnt_ready, 1)
                dve.wait_ge(tot_done, b + 2)
                step(v.tensor_scalar(inc_i, banks[0][:, 0:1], kcol, bits_f[:, bass.ds(b, 1)], ALU.is_ge, ALU.mult))
                step(v.tensor_tensor(m_i, m_i, inc_i, ALU.bitwise_or))
            link(v.tensor_tensor(thresh, m_i.bitcast(F32), sgn, ALU.mult))
            link(v.tensor_scalar(gt, wm, thresh, None, ALU.is_gt))
            v.tensor_scalar(eq, wm, thresh, None, ALU.is_equal)
            v.tensor_reduce(part, gt, AX_X, ALU.add).then_inc(mask_ready, 1)
            dve.wait_ge(prefix_done, 1)
            link(v.tensor_scalar(need, banks[1][:, 300:301], -1.0, float(TOP), ALU.mult, ALU.add))
            ranks(v, link, banks[1])
            link(v.scalar_tensor_tensor(selm, pre, need, eq, ALU.is_lt, ALU.mult))
            v.tensor_tensor(selm, selm, gt, ALU.add).then_inc(sel_set, 1)
            dve.wait_ge(prefix2_done, 1)
            ranks(v, link, banks[2])
            link(v.tensor_copy(rank_i, pre))
            v.tensor_single_scalar(r_i, rank_i, P - 1, ALU.bitwise_and)
            link(v.tensor_single_scalar(q_i, rank_i, 7, ALU.logical_shift_right))
            v.tensor_copy(r_f, r_i)
            link(v.tensor_copy(q_f, q_i))
            link(v.scalar_tensor_tensor(q_f, q_f, 1.0, selm, ALU.add, ALU.mult))
            link(v.tensor_scalar(q_f, q_f, -1.0, None, ALU.add))
            with dve.Fori(0, NS) as i:
                for h in range(2):
                    dve.wait_ge(hot_used, i * 2 + (h + 1))
                    v.tensor_scalar(hot_r[h], iota[:, :], r_f[:, bass.ds(i * 2 + h, 1)], None, ALU.is_equal)
                    v.tensor_scalar(hot_q[h], iota[:, 0:QW], q_f[:, bass.ds(i * 2 + h, 1)],
                                    tok[:, bass.ds(i * 2 + h, 1)], ALU.is_equal, ALU.mult).then_inc(hot_ready, 1)
            dve.wait_ge(ids_done, 1)
            v.tensor_copy(ids, banks[3][:, 0:QW]).then_inc(ids_ready, 1)
            dve.wait_ge(ids_ready, 1)
            link.close()

        def route_tensor(pe):
            te = nc.tensor
            pe.wait_ge(cnt_ready, 1)
            pe.wait_ge(w2_read, 2 * NS)
            te.matmul(banks[0][:, 0:1], ones[:, :], cnt, start=True, stop=True).then_inc(tot_done, 1)
            with pe.Fori(0, BITS) as b:
                pe.wait_ge(cnt_ready, b + 2)
                te.matmul(banks[0][:, 0:1], ones[:, :], cnt, start=True, stop=True).then_inc(tot_done, 1)
            pe.wait_ge(mask_ready, 1)
            te.matmul(banks[1][:, 300:301], ones[:, :], part, start=True, stop=True)
            te.matmul(banks[1][:, 0:NT], below[:, :], eq, start=True, stop=True)
            te.matmul(banks[1][:, P:P + NT], ones[:, :], eq, start=True, stop=True).then_inc(prefix_done, 1)
            pe.wait_ge(sel_set, 1)
            te.matmul(banks[2][:, 0:NT], below[:, :], selm, start=True, stop=True)
            te.matmul(banks[2][:, P:P + NT], ones[:, :], selm, start=True, stop=True).then_inc(prefix2_done, 1)
            te.matmul(banks[3][:, 0:QW], zeros[:, :], zeros[:, 0:QW], start=True, stop=False,
                      skip_group_check=True).then_inc(hot_used, 2)
            with pe.Fori(0, NS) as i:
                for h in range(2):
                    pe.wait_ge(hot_ready, i * 2 + (h + 1))
                    te.matmul(banks[3][:, 0:QW], hot_r[h], hot_q[h], start=False, stop=False,
                              skip_group_check=True).then_inc(hot_used, 1)
            te.matmul(banks[3][:, 0:QW], zeros[:, :], zeros[:, 0:QW], start=False, stop=True,
                      skip_group_check=True).then_inc(ids_done, 1)

        GN = QW // 2
        ROWS_LAST = TOP - (QT - 1) * P
        assert QT % 2 == 1 and GN % 2 == 1
        fw1 = view(resident, 2048, C, HID)
        fw2 = view(resident, 4096, HC, D)
        fb2_row = at(6144, D)
        fb1 = at(6400, HC)
        pairs = [[view(resident, 6912 + 1024 * f + 512 * j, 2, D) for j in range(2)] for f in range(2)]
        xT = [view(resident, 8960 + 512 * f, C, 2 * P) for f in range(2)]
        hT = view(resident, 9984, HC, 2 * P)
        y_row = [[at(at_ + D * j, D) for j in range(2)] for at_ in (12032, 13856)]
        o_row = [[at(12544 + 512 * f + D * j, D) for j in range(2)] for f in range(2)]
        id_stage = [at(13568 + 2 * f, 2).bitcast(I32) for f in range(2)]
        w_sel = [at(13576 + 2 * f, 2) for f in range(2)]
        w_dump = at(13600, D)
        ffn_params = sem("ffn_params")
        ids_staged, pair_landed = sem("ids_staged"), [sem(f"pair_landed{f}") for f in range(2)]
        x_turned, xT_ready, hid_done, hid_read, y_done, y_read, y_ready = (
            sem("x_turned"), sem("xT_ready"), sem("hid_done"), sem("hid_read"), sem("y_done"), sem("y_read"),
            sem("y_ready"))
        scattered = [sem(f"scattered{f}") for f in range(2)]
        w_link = sem("w_link")
        hid_banks = [banks[1], banks[2], banks[3], banks[4]]
        y_bank = qkv[:, 0].rearrange("p i s c -> p (i s c)")
        N_FFN_PARAMS = 4

        def ffn_load(act):
            act.wait_ge(h1_done, 3 * NS)
            for d, s_ in ((fw1, a["ffn_w1"].rearrange("(c p) h -> p c h", p=P)),
                          (fw2, a["ffn_w2"].rearrange("(c p) d -> p c d", p=P)),
                          (fb2_row, a["ffn_b2"].partition_broadcast(P)), (fb1, a["ffn_b1"])):
                act.dma_start(d, s_).then_inc(ffn_params, 16)

        def ffn_pool(pool):
            stage, done = pool.alloc_register("stage_f"), pool.alloc_register("done_f")
            pool.reg_mov(stage, 1)
            pool.reg_mov(done, 1)

            def gather(g, f):
                if isinstance(g, int):
                    pool.wait_ge(ids_staged, g + 1)
                else:
                    counted(pool, ids_staged, stage)
                for j in range(2):
                    nc.gpsimd.indirect_dma_start(
                        out=pairs[f][j].rearrange("p a d -> p (a d)"), out_offset=None, in_=pair_dram[:, :],
                        in_offset=bass.IndirectOffsetOnAxis(ap=id_stage[f][:, j:j + 1], axis=0)
                    ).then_inc(pair_landed[f], 16)

            def scatter(g, f, tiles=2, n=P):
                if isinstance(g, int):
                    pool.wait_ge(y_ready, g + 1)
                else:
                    counted(pool, y_ready, done)
                for j in range(tiles):
                    nc.gpsimd.indirect_dma_start(
                        out=out[:, :], out_offset=bass.IndirectOffsetOnAxis(ap=id_stage[f][:n, j:j + 1], axis=0),
                        in_=o_row[f][j][:n], in_offset=None).then_inc(scattered[f], 16)

            for h in range(2):
                pool.wait_ge(pair_stored[h], 16 * NS)
                pool.wait_ge(base_stored[h], 16 * NS)
            gather(0, 0)
            gather(1, 1)
            pool.reg_mov(stage, 3)
            with pool.Fori(0, (GN - 3) // 2) as u:
                for f in range(2):
                    scatter(u * 2 + f, f)
                    gather(u * 2 + f, f)
            scatter(GN - 3, 0)
            gather(GN - 1, 0)
            scatter(GN - 2, 1)
            scatter(GN - 1, 0, tiles=1, n=ROWS_LAST)
            pool.wait_ge(scattered[0], 32 * (GN // 2) + 16)
            pool.wait_ge(scattered[1], 32 * (GN // 2))

        def ffn_scalar(act):
            s = nc.scalar

            def turned(g, f):
                act.wait_ge(x_turned, g + 1)
                after(act, hid_done, g * 4 - 4)
                s.activation(xT[f].rearrange("p c n -> p (c n)"), banks[0][:, :], ACT.Copy).then_inc(xT_ready, 1)

            def hidden(g):
                after(act, y_done, g)
                for q in range(4):
                    act.wait_ge(hid_done, g * 4 + (q + 1))
                    for e in range(2):
                        k = 2 * q + e
                        ins = s.activation(hT[:, k], hid_banks[q][:, e * D:(e + 1) * D], ACT.Gelu_apprx_tanh,
                                           bias=fb1[:, k:k + 1])
                    ins.then_inc(hid_read, 1)

            act.wait_ge(ffn_params, 16 * N_FFN_PARAMS)
            turned(0, 0)
            for g in range(2):
                hidden(g)
                turned(g + 1, 1 - g)
            with act.Fori(1, GN // 2) as u:
                for f in range(2):
                    hidden(u * 2 + f)
                    turned(u * 2 + (f + 1), 1 - f)
            hidden(GN - 1)

        def ffn_vector(dve):
            v = nc.vector

            def stage(g, f):
                if not (isinstance(g, int) and g < 2):
                    dve.wait_ge(scattered[f], g * 16 - 16 * f)
                v.tensor_copy(id_stage[f], ids[:, bass.ds(g * 2, 2)]).then_inc(ids_staged, 1)

            def weigh(g, f):
                dve.wait_ge(pair_landed[f], g * 16 + (32 - 16 * f))
                link = Link(dve, w_link, 2, g)
                for j in range(2):
                    link(v.tensor_tensor_reduce(w_dump, pairs[f][j][:, 1], wr_row[:, :], 1.0, 0.0, ALU.mult, ALU.add,
                                                w_sel[f][:, j:j + 1]))
                v.tensor_scalar(w_sel[f], w_sel[f], br_col, None, ALU.add).then_inc(w_ready, 1)

            def result(g, f):
                dve.wait_ge(y_done, g + 1)
                dve.wait_ge(w_ready, g + 1)
                for j in range(2):
                    ins = v.tensor_tensor(y_row[f][j], y_bank[:, j * D:(j + 1) * D], fb2_row, ALU.add)
                ins.then_inc(y_read, 1)
                dve.wait_ge(y_read, g + 1)
                for j in range(2):
                    ins = v.scalar_tensor_tensor(o_row[f][j], y_row[f][j], w_sel[f][:, j:j + 1], pairs[f][j][:, 0],
                                                 ALU.mult, ALU.add)
                ins.then_inc(y_ready, 1)

            dve.wait_ge(ffn_params, 16 * N_FFN_PARAMS)
            stage(0, 0)
            stage(1, 1)
            weigh(0, 0)
            with dve.Fori(0, (GN - 3) // 2) as u:
                for f in range(2):
                    g = u * 2 + f
                    weigh(g + 1, 1 - f)
                    result(g, f)
                    stage(g + 2, f)
            weigh(GN - 2, 1)
            result(GN - 3, 0)
            stage(GN - 1, 0)
            weigh(GN - 1, 0)
            result(GN - 2, 1)
            result(GN - 1, 0)

        w_ready = sem("w_ready")

        def ffn_tensor(pe):
            te = nc.tensor

            def turn(g, f):
                pe.wait_ge(pair_landed[f], g * 16 + (32 - 16 * f))
                after(pe, xT_ready, g)
                for c in range(C):
                    for j in range(2):
                        ins = te.transpose(banks[0][:, (c * 2 + j) * P:(c * 2 + j + 1) * P],
                                           pairs[f][j][:, 1, c * P:(c + 1) * P], ident[:, :])
                ins.then_inc(x_turned, 1)

            def hidden(g, f):
                pe.wait_ge(xT_ready, g + 1)
                for q in range(4):
                    after(pe, hid_read, g * 4 + (q - 3))
                    for e in range(2):
                        k = 2 * q + e
                        for c in range(C):
                            ins = te.matmul(hid_banks[q][:, e * D:(e + 1) * D], fw1[:, c, k * P:(k + 1) * P], xT[f][:, c],
                                            start=(c == 0), stop=(c == C - 1))
                    ins.then_inc(hid_done, 1)

            def project(g):
                pe.wait_ge(hid_read, g * 4 + 4)
                after(pe, y_read, g)
                for j in range(2):
                    for k in range(HC):
                        ins = te.matmul(y_bank[:, j * D:(j + 1) * D], hT[:, k, j * P:(j + 1) * P], fw2[:, k],
                                        start=(k == 0), stop=(k == HC - 1))
                ins.then_inc(y_done, 1)

            pe.wait_ge(ffn_params, 16 * N_FFN_PARAMS)
            turn(0, 0)
            hidden(0, 0)
            turn(1, 1)
            project(0)
            hidden(1, 1)
            turn(2, 0)
            project(1)
            with pe.Fori(1, GN // 2) as u:
                for f in range(2):
                    hidden(u * 2 + f, f)
                    turn(u * 2 + (f + 1), 1 - f)
                    project(u * 2 + f)
            hidden(GN - 1, 0)
            project(GN - 1)

        @block.sync
        def _(sp):
            tables_sync(sp)
            norm_sync(sp)
            main_sync(sp)

        @block.gpsimd
        def _(pool):
            tables_pool(pool)
            main_pool(pool)
            route_pool(pool)
            ffn_pool(pool)

        @block.scalar
        def _(act):
            params_act(act)
            norm_scalar(act)
            bn_scalar(act)
            main_scalar(act)
            ffn_load(act)
            ffn_scalar(act)

        @block.vector
        def _(dve):
            tables_vector(dve)
            stats_turn = dve.alloc_register("stats_turn")
            dve.reg_mov(stats_turn, 1)
            norm_vector(dve, stats_turn)
            bn_vector(dve)
            main_vector(dve, stats_turn)
            route_vector(dve)
            ffn_vector(dve)

        @block.tensor
        def _(pe):
            tables_tensor(pe)
            norm_tensor(pe)
            bn_tensor(pe)
            main_tensor(pe)
            route_tensor(pe)
            ffn_tensor(pe)


def kernel(**inputs):
    import concourse.bacc as bacc
    from concourse.bass_utils import run_bass_kernel_spmd

    A = {k: np.ascontiguousarray(v) for k, v in inputs.items()}

    def roles(w, axis):
        s = w.shape
        w = w.reshape(s[:axis] + (8, 3, 32) + s[axis + 1:])
        return np.swapaxes(w, axis, axis + 1).reshape(s)

    w_pw = roles(A["L0_mix_w_pw"][:, :, 0], 0).reshape(6, 4, 32, 32)
    w_res = A["L0_mix_w_res"][:, :, 0].reshape(D, 2, 2, 4, 32)
    laid = {
        "x": A["x"], "src": A["src"], "dst": A["dst"], "edge_weight": A["edge_weight"],
        "wqkvT": roles(A["L0_mix_w_qkv"], 0).transpose(2, 1, 0),
        "gamma": roles(A["L0_mix_bn_gamma"], 0).reshape(6, P).T,
        "beta": roles(A["L0_mix_bn_beta"], 0).reshape(6, P).T,
        "w_dw": roles(A["L0_mix_w_dw"][:, 0, :], 0).reshape(6, P, 5).transpose(2, 1, 0),
        "w_pw": w_pw.transpose(1, 3, 0, 2),
        "wresT": w_res.transpose(2, 1, 3, 4, 0).reshape(512, D),
        "b_res": A["L0_mix_b_res"],
        "W1T": A["L0_gnn_W1"].T, "W2T": A["L0_gnn_W2"].T,
        "b1": A["L0_gnn_b1"].reshape(2, P).T, "b2": A["L0_gnn_b2"], "eps": A["L0_gnn_eps"],
        "wr": A["L0_ffn_wr"].reshape(D), "br": A["L0_ffn_br"],
        "ffn_w1": A["L0_ffn_w1"], "ffn_w2": A["L0_ffn_w2"],
        "ffn_b1": A["L0_ffn_b1"].reshape(HC, P).T, "ffn_b2": A["L0_ffn_b2"],
    }
    nc = bacc.Bacc("TRN2", target_bir_lowering=False, num_devices=1)
    arrays, args = {}, {}
    for name, arr in laid.items():
        arr = np.ascontiguousarray(arr)
        arrays["in_" + name] = arr
        args[name] = nc.dram_tensor("in_" + name, arr.shape, mybir.dt.from_np(arr.dtype), kind="ExternalInput").ap()
    out = nc.dram_tensor("out", A["x"].shape, F32, kind="ExternalOutput").ap()
    build(nc, args, out)
    r = run_bass_kernel_spmd(nc, [arrays], core_ids=[0])
    return r.results[0]["out"]
```
